# Optimizing a Trainium2 kernel written in Bass

```python
import numpy as np
import jax
import jax.numpy as jnp

def _softmax(x, axis=-1):
    return jax.nn.softmax(x, axis=axis)

def _gelu(x):
    return jax.nn.gelu(x, approximate=True)

def _silu(x):
    return jax.nn.silu(x)

def _sigmoid(x):
    return jax.nn.sigmoid(x)

def _layernorm(x, axis=-1, eps=1e-05):
    m = jnp.mean(x, axis=axis, keepdims=True)
    v = jnp.var(x, axis=axis, keepdims=True)
    return (x - m) / jnp.sqrt(v + eps)

def _scatter_add(tgt, idx, src, axis=0):
    return tgt.at[idx].add(src)

def _segment_sum(src, seg, n):
    return jax.ops.segment_sum(src, seg, n)
kernel_name = 'mk_flamingo_gated_d1_seqx_r8_c47ffd'

def setup_inputs(seed: int=0):
    np.random.seed(seed)
    _w = jnp.asarray

    def _rec_inputs():
        import jax
        import jax.numpy as jnp
        _rk = jax.random.key(seed)
        x = -0.0002928 + 1 * jax.random.normal(jax.random.fold_in(_rk, 1), (16, 256, 128), jnp.float32)
        _lenS = 256 - jax.random.randint(jax.random.fold_in(_rk, 7), (16,), 0, max(1, 256 // 4) + 1, jnp.int32)
        _lenS2 = 1601 - jax.random.randint(jax.random.fold_in(_rk, 8), (16,), 0, max(1, 1601 // 4) + 1, jnp.int32)
        _ctx_1024P = jax.random.normal(jax.random.fold_in(_rk, 11), (16, 16, 128), jnp.float32)
        _ctx_1024c = jax.random.dirichlet(jax.random.fold_in(_rk, 511), 0.3 * jnp.ones((16,), jnp.float32), (16, 1601))
        _ctx_1024t = jnp.einsum('bsk,bkd->bsd', _ctx_1024c, _ctx_1024P)
        _ctx_1024t = _ctx_1024t * jax.lax.rsqrt(jnp.mean(jnp.square(_ctx_1024t)) + 1e-12) * 0.953939
        ctx_1024 = -1.39393e-06 + 0.999914 * (_ctx_1024t + 0.3 * jax.random.normal(jax.random.fold_in(_rk, 611), (16, 1601, 128), jnp.float32))
        _validS = jnp.arange(256)[None, :] < _lenS[:, None]
        _validS2 = jnp.arange(1601)[None, :] < _lenS2[:, None]
        _causal = jnp.tril(jnp.ones((256, 256), dtype=bool))
        mask_Bx1xSxS2_bk1 = jnp.broadcast_to(_validS2[:, None, None, :], (16, 1, 256, 1601))
        _g = jax.random.normal(jax.random.fold_in(_rk, 9001), (2, 1), jnp.float32)
        _g = jnp.sign(_g) * jnp.maximum(jnp.abs(_g), 1.0) + (_g == 0) * 1.0
        g_xattn = _g[0]
        g_ffn = _g[1]
        return (x, ctx_1024, mask_Bx1xSxS2_bk1, g_xattn, g_ffn)
    x, ctx_1024, mask_Bx1xSxS2_bk1, g_xattn, g_ffn = _rec_inputs()

    def _L0_xattn_setup():
        import jax, jax.numpy as jnp
        import numpy as np
        D_MODEL = 128
        NUM_HEADS = 16
        D_K = D_MODEL // NUM_HEADS
        B, S = (2, 256)
        NEG = -1000000000.0

        def _split_heads(x):
            b, s, _ = x.shape
            return x.reshape(b, s, NUM_HEADS, D_K).transpose(0, 2, 1, 3)
        key = jax.random.key(seed)
        ks = jax.random.split(key, 12)
        scale = 1.0 / np.sqrt(D_MODEL)
        inp = {'q': jax.random.normal(ks[0], (B, S, D_MODEL), jnp.float32), 'k': jax.random.normal(ks[1], (B, S, D_MODEL), jnp.float32), 'v': jax.random.normal(ks[2], (B, S, D_MODEL), jnp.float32), 'mask': jax.random.randint(ks[3], (B, 1, S, S), 0, 2) == 1, 'w_q': jax.random.normal(ks[4], (D_MODEL, D_MODEL), jnp.float32) * scale, 'b_q': jnp.zeros((D_MODEL,), jnp.float32), 'w_k': jax.random.normal(ks[5], (D_MODEL, D_MODEL), jnp.float32) * scale, 'b_k': jnp.zeros((D_MODEL,), jnp.float32), 'w_v': jax.random.normal(ks[6], (D_MODEL, D_MODEL), jnp.float32) * scale, 'b_v': jnp.zeros((D_MODEL,), jnp.float32), 'w_o': jax.random.normal(ks[7], (D_MODEL, D_MODEL), jnp.float32) * scale, 'b_o': jnp.zeros((D_MODEL,), jnp.float32)}
        return inp
    _L0_xattn_all = _L0_xattn_setup()
    _L0_xattn_in = {k: v for k, v in _L0_xattn_all.items() if k in ('w_q', 'b_q', 'w_k', 'b_k', 'w_v', 'b_v', 'w_o', 'b_o')}
    del _L0_xattn_all

    def _L0_ffn_setup():
        import jax, jax.numpy as jnp
        import numpy as np
        DIM = 128
        DEPTH = 6
        HEADS = 16
        DIM_HEAD = 64
        WINDOW = 32
        INNER = HEADS * DIM_HEAD
        DIM_INNER = int(DIM * 4 * 2 / 3)
        QK_SCALE = 8.0

        def shift_tokens(t):
            a, s = jnp.split(t, 2, -1)
            s = jnp.pad(s, ((0, 0), (1, 0), (0, 0)))[:, :-1]
            return jnp.concatenate([a, s], -1)

        def l2norm(t):
            return t / jnp.maximum(jnp.linalg.norm(t, axis=-1, keepdims=True), 1e-12)

        def rotate_half(x):
            x1, x2 = jnp.split(x, 2, -1)
            return jnp.concatenate([-x2, x1], -1)

        def rotary_tables(n):
            half = jnp.arange(0, DIM_HEAD, 2, dtype=jnp.float32)
            inv_freq = 1.0 / 10000.0 ** (half / DIM_HEAD)
            t = jnp.arange(n, dtype=jnp.float32)
            freqs = t[:, None] * inv_freq[None, :]
            freqs = jnp.concatenate([freqs, freqs], -1)
            base_scale = (half + 0.4 * DIM_HEAD) / (1.4 * DIM_HEAD)
            power = (t - n // 2) / (WINDOW // 2)
            scale = base_scale[None, :] ** power[:, None]
            scale = jnp.concatenate([scale, scale], -1)
            return (freqs, scale)

        def local_attention(q, k, v):
            b, h, n, d = q.shape
            w = WINDOW
            nw = n // w
            bq = q.reshape(b, h, nw, w, d)
            bk = k.reshape(b, h, nw, w, d)
            bv = v.reshape(b, h, nw, w, d)

            def look(t):
                p = jnp.pad(t, ((0, 0), (0, 0), (1, 0), (0, 0), (0, 0)))
                return jnp.concatenate([p[:, :, :nw], p[:, :, 1:]], axis=3)
            bk2, bv2 = (look(bk), look(bv))
            seq = jnp.arange(n).reshape(nw, w)
            seq_p = jnp.pad(seq, ((1, 0), (0, 0)), constant_values=-1)
            jt = jnp.concatenate([seq_p[:nw], seq_p[1:]], axis=1)
            it = seq[:, :, None]
            jb = jt[:, None, :]
            mask = (it < jb) | (it > jb + w) | (jb == -1)
            sim = jnp.einsum('bhwie,bhwje->bhwij', bq, bk2) * QK_SCALE
            sim = jnp.where(mask, -jnp.finfo(sim.dtype).max, sim)
            attn = jax.nn.softmax(sim, -1)
            out = jnp.einsum('bhwij,bhwje->bhwie', attn, bv2)
            return out.reshape(b, h, n, d)

        def attn_layer(x, Wqkv, qs, ksc, Wo):
            b, n, _ = x.shape
            qkv = x @ Wqkv
            q, k, v = jnp.split(qkv, 3, -1)
            sh = lambda t: t.reshape(b, n, HEADS, DIM_HEAD).transpose(0, 2, 1, 3)
            q, k, v = (sh(q), sh(k), sh(v))
            q = l2norm(q) * qs
            k = l2norm(k) * ksc
            freqs, scale = rotary_tables(n)
            cos, sin = (jnp.cos(freqs), jnp.sin(freqs))
            q = q * cos * scale + rotate_half(q) * sin * scale
            inv = 1.0 / scale
            k = k * cos * inv + rotate_half(k) * sin * inv
            out = local_attention(q, k, v)
            out = out.transpose(0, 2, 1, 3).reshape(b, n, INNER)
            return out @ Wo

        def ffn_layer(x, g, bln, W1, b1, W2, b2):
            mu = x.mean(-1, keepdims=True)
            var = ((x - mu) ** 2).mean(-1, keepdims=True)
            xn = (x - mu) / jnp.sqrt(var + 1e-05) * g + bln
            hg = xn @ W1 + b1
            a, gate = jnp.split(hg, 2, -1)
            return a * jax.nn.gelu(gate, approximate=False) @ W2 + b2
        key = jax.random.key(seed)
        ks = jax.random.split(key, 8)
        B, N = (2, 256)
        init = lambda k, shape: jax.random.normal(k, shape, jnp.float32) * 0.02
        return {'x': jax.random.normal(ks[0], (B, N, DIM), jnp.float32), 'Wqkv': init(ks[1], (DEPTH, DIM, 3 * INNER)), 'q_scale': jnp.ones((DEPTH, DIM_HEAD), jnp.float32), 'k_scale': jnp.ones((DEPTH, DIM_HEAD), jnp.float32), 'Wo': init(ks[2], (DEPTH, INNER, DIM)), 'ln_g': jnp.ones((DEPTH, DIM), jnp.float32), 'ln_b': jnp.zeros((DEPTH, DIM), jnp.float32), 'W1': init(ks[3], (DEPTH, DIM, 2 * DIM_INNER)), 'b1': jnp.zeros((DEPTH, 2 * DIM_INNER), jnp.float32), 'W2': init(ks[4], (DEPTH, DIM_INNER, DIM)), 'b2': jnp.zeros((DEPTH, DIM), jnp.float32)}
    _L0_ffn_all = _L0_ffn_setup()
    _L0_ffn_in = {k: v for k, v in _L0_ffn_all.items() if k in ('Wqkv', 'q_scale', 'k_scale', 'Wo', 'ln_g', 'ln_b', 'W1', 'b1', 'W2', 'b2')}
    del _L0_ffn_all
    return {'x': x, 'ctx_1024': ctx_1024, 'mask_Bx1xSxS2_bk1': mask_Bx1xSxS2_bk1, 'g_xattn': g_xattn, 'g_ffn': g_ffn, 'L0_xattn_w_q': _L0_xattn_in['w_q'], 'L0_xattn_b_q': _L0_xattn_in['b_q'], 'L0_xattn_w_k': _L0_xattn_in['w_k'], 'L0_xattn_b_k': _L0_xattn_in['b_k'], 'L0_xattn_w_v': _L0_xattn_in['w_v'], 'L0_xattn_b_v': _L0_xattn_in['b_v'], 'L0_xattn_w_o': _L0_xattn_in['w_o'], 'L0_xattn_b_o': _L0_xattn_in['b_o'], 'L0_ffn_Wqkv': _L0_ffn_in['Wqkv'], 'L0_ffn_q_scale': _L0_ffn_in['q_scale'], 'L0_ffn_k_scale': _L0_ffn_in['k_scale'], 'L0_ffn_Wo': _L0_ffn_in['Wo'], 'L0_ffn_ln_g': _L0_ffn_in['ln_g'], 'L0_ffn_ln_b': _L0_ffn_in['ln_b'], 'L0_ffn_W1': _L0_ffn_in['W1'], 'L0_ffn_b1': _L0_ffn_in['b1'], 'L0_ffn_W2': _L0_ffn_in['W2'], 'L0_ffn_b2': _L0_ffn_in['b2']}

def reference(x, ctx_1024, mask_Bx1xSxS2_bk1, g_xattn, g_ffn, L0_xattn_w_q, L0_xattn_b_q, L0_xattn_w_k, L0_xattn_b_k, L0_xattn_w_v, L0_xattn_b_v, L0_xattn_w_o, L0_xattn_b_o, L0_ffn_Wqkv, L0_ffn_q_scale, L0_ffn_k_scale, L0_ffn_Wo, L0_ffn_ln_g, L0_ffn_ln_b, L0_ffn_W1, L0_ffn_b1, L0_ffn_W2, L0_ffn_b2):
    import jax
    import jax.numpy as jnp

    def _L0_xattn_ref(q, k, v, mask, w_q, b_q, w_k, b_k, w_v, b_v, w_o, b_o):
        import jax, jax.numpy as jnp
        import numpy as np
        D_MODEL = 128
        NUM_HEADS = 16
        D_K = D_MODEL // NUM_HEADS
        B, S = (2, 256)
        NEG = -1000000000.0

        def _split_heads(x):
            b, s, _ = x.shape
            return x.reshape(b, s, NUM_HEADS, D_K).transpose(0, 2, 1, 3)
        qh = _split_heads(q @ w_q + b_q)
        kh = _split_heads(k @ w_k + b_k)
        vh = _split_heads(v @ w_v + b_v)
        scores = jnp.einsum('bhqd,bhkd->bhqk', qh, kh) / jnp.sqrt(jnp.asarray(D_K, jnp.float32))
        scores = jnp.where(mask, NEG, scores)
        attn = jax.nn.softmax(scores, axis=-1)
        out = jnp.einsum('bhqk,bhkd->bhqd', attn, vh)
        out = out.transpose(0, 2, 1, 3).reshape(q.shape[0], -1, D_MODEL)
        return out @ w_o + b_o

    def _L0_ffn_ref(x, Wqkv, q_scale, k_scale, Wo, ln_g, ln_b, W1, b1, W2, b2):
        import jax, jax.numpy as jnp
        import numpy as np
        DIM = 128
        DEPTH = 6
        HEADS = 16
        DIM_HEAD = 64
        WINDOW = 32
        INNER = HEADS * DIM_HEAD
        DIM_INNER = int(DIM * 4 * 2 / 3)
        QK_SCALE = 8.0

        def shift_tokens(t):
            a, s = jnp.split(t, 2, -1)
            s = jnp.pad(s, ((0, 0), (1, 0), (0, 0)))[:, :-1]
            return jnp.concatenate([a, s], -1)

        def l2norm(t):
            return t / jnp.maximum(jnp.linalg.norm(t, axis=-1, keepdims=True), 1e-12)

        def rotate_half(x):
            x1, x2 = jnp.split(x, 2, -1)
            return jnp.concatenate([-x2, x1], -1)

        def rotary_tables(n):
            half = jnp.arange(0, DIM_HEAD, 2, dtype=jnp.float32)
            inv_freq = 1.0 / 10000.0 ** (half / DIM_HEAD)
            t = jnp.arange(n, dtype=jnp.float32)
            freqs = t[:, None] * inv_freq[None, :]
            freqs = jnp.concatenate([freqs, freqs], -1)
            base_scale = (half + 0.4 * DIM_HEAD) / (1.4 * DIM_HEAD)
            power = (t - n // 2) / (WINDOW // 2)
            scale = base_scale[None, :] ** power[:, None]
            scale = jnp.concatenate([scale, scale], -1)
            return (freqs, scale)

        def local_attention(q, k, v):
            b, h, n, d = q.shape
            w = WINDOW
            nw = n // w
            bq = q.reshape(b, h, nw, w, d)
            bk = k.reshape(b, h, nw, w, d)
            bv = v.reshape(b, h, nw, w, d)

            def look(t):
                p = jnp.pad(t, ((0, 0), (0, 0), (1, 0), (0, 0), (0, 0)))
                return jnp.concatenate([p[:, :, :nw], p[:, :, 1:]], axis=3)
            bk2, bv2 = (look(bk), look(bv))
            seq = jnp.arange(n).reshape(nw, w)
            seq_p = jnp.pad(seq, ((1, 0), (0, 0)), constant_values=-1)
            jt = jnp.concatenate([seq_p[:nw], seq_p[1:]], axis=1)
            it = seq[:, :, None]
            jb = jt[:, None, :]
            mask = (it < jb) | (it > jb + w) | (jb == -1)
            sim = jnp.einsum('bhwie,bhwje->bhwij', bq, bk2) * QK_SCALE
            sim = jnp.where(mask, -jnp.finfo(sim.dtype).max, sim)
            attn = jax.nn.softmax(sim, -1)
            out = jnp.einsum('bhwij,bhwje->bhwie', attn, bv2)
            return out.reshape(b, h, n, d)

        def attn_layer(x, Wqkv, qs, ksc, Wo):
            b, n, _ = x.shape
            qkv = x @ Wqkv
            q, k, v = jnp.split(qkv, 3, -1)
            sh = lambda t: t.reshape(b, n, HEADS, DIM_HEAD).transpose(0, 2, 1, 3)
            q, k, v = (sh(q), sh(k), sh(v))
            q = l2norm(q) * qs
            k = l2norm(k) * ksc
            freqs, scale = rotary_tables(n)
            cos, sin = (jnp.cos(freqs), jnp.sin(freqs))
            q = q * cos * scale + rotate_half(q) * sin * scale
            inv = 1.0 / scale
            k = k * cos * inv + rotate_half(k) * sin * inv
            out = local_attention(q, k, v)
            out = out.transpose(0, 2, 1, 3).reshape(b, n, INNER)
            return out @ Wo

        def ffn_layer(x, g, bln, W1, b1, W2, b2):
            mu = x.mean(-1, keepdims=True)
            var = ((x - mu) ** 2).mean(-1, keepdims=True)
            xn = (x - mu) / jnp.sqrt(var + 1e-05) * g + bln
            hg = xn @ W1 + b1
            a, gate = jnp.split(hg, 2, -1)
            return a * jax.nn.gelu(gate, approximate=False) @ W2 + b2
        for i in range(DEPTH):
            x = attn_layer(shift_tokens(x), Wqkv[i], q_scale[i], k_scale[i], Wo[i]) + x
            x = ffn_layer(shift_tokens(x), ln_g[i], ln_b[i], W1[i], b1[i], W2[i], b2[i]) + x
        return x
    x = x + jnp.tanh(g_xattn[0]) * _L0_xattn_ref(_layernorm(x, axis=-1), ctx_1024, ctx_1024, mask_Bx1xSxS2_bk1, L0_xattn_w_q, L0_xattn_b_q, L0_xattn_w_k, L0_xattn_b_k, L0_xattn_w_v, L0_xattn_b_v, L0_xattn_w_o, L0_xattn_b_o)
    x = x + jnp.tanh(g_ffn[0]) * _L0_ffn_ref(_layernorm(x, axis=-1), L0_ffn_Wqkv, L0_ffn_q_scale, L0_ffn_k_scale, L0_ffn_Wo, L0_ffn_ln_g, L0_ffn_ln_b, L0_ffn_W1, L0_ffn_b1, L0_ffn_W2, L0_ffn_b2)
    return x

_drawn_inputs = setup_inputs


def setup_inputs(seed=0):
    import zlib

    import numpy as np

    out = dict(_drawn_inputs(seed))
    spreads = {'L0_xattn_b_q': (0.0, 0.437),
     'L0_xattn_b_k': (0.0, 2.0),
     'L0_xattn_b_v': (0.0, 0.1),
     'L0_xattn_b_o': (0.0, 0.1),
     'L0_ffn_q_scale': (1.0, 0.2),
     'L0_ffn_k_scale': (1.0, 0.546),
     'L0_ffn_ln_g': (1.0, 0.6),
     'L0_ffn_ln_b': (0.0, 0.749),
     'L0_ffn_b1': (0.0, 0.1),
     'L0_ffn_b2': (0.0, 0.1)}
    factors = {}
    for name, (base, spread) in spreads.items():
        noise = np.random.default_rng([zlib.crc32(name.encode()), seed]).standard_normal(out[name].shape)
        drawn = base * np.exp(spread * noise) if base else spread * noise
        out[name] = jnp.asarray(drawn.astype(out[name].dtype))
    for name, factor in factors.items():
        out[name] = (out[name] * factor).astype(out[name].dtype)
    return out
```

```python
from contextlib import ExitStack

import numpy as np

import concourse.bass as bass
from concourse import mybir

F32 = mybir.dt.float32
BF16 = mybir.dt.bfloat16
U8 = mybir.dt.uint8
ALU = mybir.AluOpType
ACT = mybir.ActivationFunctionType
AX_X = mybir.AxisListType.X

P = 128
S = 256
INNER, DH = 1024, 64
WIN = 32
QK_SCALE = 8.0
KW = WIN + P
NJ = INNER // P
FFN = 341
FB = 3
BIG = float(2 ** 100)
W_QK, W_V, W_O = 0, 2 * INNER, 3 * INNER
W_1 = 4 * INNER
W_2 = W_1 + 2 * FB * P
W_END = W_2 + FB * P
W_PARTS = ((0, INNER), (INNER, W_V), (W_V, W_O), (W_O, W_1), (W_1, W_2), (W_2, W_END))
PART_Q, PART_K, PART_V, PART_O, PART_1, PART_2 = range(6)
P_Q, P_QR, P_K, P_KR, P_G, P_B, P_B2, P_B1 = range(8)
N_PAR = P_B1 + 2 * FB
STEPS = 8
GMAX = 3
GROUPS = [(t, j0, n) for t in range(2) for j0, n in ((0, 3), (3, 3), (6, 2))]
PAD = P - WIN
LN_SCALE = float(2 ** 20)
AHEAD = 2


HX, DK = 16, 8
KEYS = 1601
KT = -(-KEYS // P)
S_UNITS = [range(2 * i, 2 * i + 2) for i in range(8)]
LOWEST = -3.0e38
XW_Q, XW_K, XW_V, XW_O = 0, P, 2 * P, 3 * P
XW_M = XW_O + 4 * P
XW_S = XW_M + P
X_END = XW_S + P
XV_BQ, XV_BK, XV_BO, XV_G = range(4)
X_NVEC = 4
N_SETX = 8


EXP_LN_TABLES = 6


def load_tables(nc, act, tables):
    act.add_instruction(mybir.InstLoadActFuncSet(name=nc.get_next_instruction_name(),
                                                 engine=mybir.EngineType.Activation, act_func_set_id=tables))


def wait_apart(eng, passed, sem, value):
    eng.wait_ge(sem, value)
    eng.sem_inc(passed, 1)


def cross_phase(nc, x1_scr, xn_scr, ident, identb, ins, NB):
    with ExitStack() as ctx:
        def sb(name, shape, dt=F32):
            return ctx.enter_context(nc.sbuf_tensor(name, shape, dt))

        def sem(name):
            return ctx.enter_context(nc.semaphore(name))

        w_sb = sb("w_sb", [P, X_END])
        vec = sb("vec", [P, X_NVEC])
        bv = sb("bv", [P, P])
        gate_x = sb("gate_x", [P, 1])
        ctxT = sb("ctxT", [P, KEYS])
        kf = sb("kf", [P, KEYS])
        kp = sb("kp", [P, 3, KEYS], BF16)
        qf = sb("qf", [P, S])
        qp = sb("qp", [P, 3, S], BF16)
        k_op = [sb(f"k_op{i}", [P, 4, KEYS], BF16) for i in range(4)]
        q_max = sb("q_max", [P, 2, HX, S], BF16)
        q_exp = sb("q_exp", [P, 2, HX, S], BF16)
        onesr = sb("onesr", [3, KEYS], BF16)
        vx = sb("vx", [P, 2, KT, HX, DK + 1])
        m8 = sb("m8", [P, 2, KEYS], U8)
        mt8 = sb("mt8", [P, KT, S], U8)
        mq = sb("mq", [P, 2, 2, KEYS], BF16)
        mk = sb("mk", [P, 2, KT, S], BF16)
        junk = sb("junk", [P, 2, 1024], BF16)
        smax = sb("smax", [P, 2, 8])
        smax1 = sb("smax1", [P, 8])
        mneg = sb("mneg", [4, S])
        mres = sb("mres", [4, S])
        mres2 = sb("mres2", [4, S])
        mp = sb("mp", [4, 3, S], BF16)
        eT = sb("eT", [P, 2, 4 * S])
        u4 = sb("u4", [P, 4, S])
        ru = sb("ru", [P, 4, S])
        t1 = sb("t1", [P, S])
        y1 = sb("y1", [P, S])
        lc = sb("lc", [P, 2, S])
        lsq = sb("lsq", [P, 2, S])
        lve = sb("lve", [P, 2, S])
        lln = sb("lln", [P, 2, S])
        lrs = sb("lrs", [P, 2, S])
        xq = sb("xq", [P, S])
        xa = sb("xa", [P, S])
        xb = sb("xb", [P, S])
        xn = sb("xn_x", [P, S])
        k_scr = nc.dram_tensor("k_scr", [2, 3, P, KEYS], BF16, kind="Internal").ap()
        q_scr = nc.dram_tensor("q_scr", [2, 3, P, S], BF16, kind="Internal").ap()

        b_s = [ctx.enter_context(nc.psum_tensor(f"b_s{i}", [P, 1024], F32)) for i in range(2)]
        b_e = [ctx.enter_context(nc.psum_tensor(f"b_e{i}", [P, 512], F32)) for i in range(2)]
        b_pv = ctx.enter_context(nc.psum_tensor("b_pv", [P, 512], F32))
        b_p = ctx.enter_context(nc.psum_tensor("b_p", [P, 512], F32))

        per = dict(e_done=8 * KT, e_ready=8 * KT, pv_done=4 * KT, u_kept=4, s_done=64, s_max=64, mx_ready=4,
                   mneg_ready=4, mhi_ready=4, mres_ready=4, mmid_ready=4, mres2_ready=4, mp_ready=4,
                   kf_ready=4, khi_ready=1, kres_ready=1, kmid_ready=1, klo_ready=1, vx_ready=4,
                   qf_ready=1, qhi_ready=1, qres_ready=1, qmid_ready=1, qlo_ready=1,
                   mq_ready=1, mk_ready=1, xq_ready=1, sums_kept=2, ru_ready=4, un_ready=2, t1_ready=1, y1_ready=1,
                   xn_ready=1, lcq_ready=1, lsqq_ready=1, lveq_ready=1, llnq_ready=1, lrsq_ready=1,
                   lcy_ready=1, lsqy_ready=1, lvey_ready=1, llny_ready=1, lrsy_ready=1)
        pe_own = ("e_done", "pv_done", "s_done")
        act_own = ("e_ready", "kf_ready", "khi_ready", "kmid_ready", "qhi_ready", "qmid_ready", "llnq_ready", "lrsq_ready",
                   "llny_ready", "lrsy_ready")
        pool_own = ("mq_ready", "mk_ready")
        dma_per = dict(xa_in=16, xb_in=16, x1_kept=16, xn_kept=16, ctx_in=16, m8_in=16, mt8_in=32, kscr_in=48, qscr_in=48, qop_in=18 * 16, mrow_in=4 * 48)
        s = {n: sem(n) for n in (*per, *dma_per)}
        per.update(dma_per)
        kop_in = [sem(f"kop_in{i}") for i in range(4)]
        KOP = 9 * 16
        pool_passed = sem("pool_passed_x")
        dve_passed = sem("dve_passed_x")
        start_in = sem("start_in")
        set_pool = sem("set_pool")
        set_dve = sem("set_dve")
        ones_in = sem("ones_in")
        gate_ready = sem("gate_ready_x")
        bank_filled = sem("bank_filled")

        def last_reader(kind, j, row):
            name, c = dict(max=("mneg_ready", max_index(j)), k=("kf_ready", j + 1), v=("vx_ready", j + 1),
                           q=("qf_ready", 1), mean_q=("lcq_ready", 1), mean_y=("lcy_ready", 1),
                           var_q=("lveq_ready", 1), var_y=("lvey_ready", 1), sums=("sums_kept", j + 1),
                           out=("t1_ready", 1))[kind]
            return s[name], count(name, row[0], c)

        def row_of(kind, j, cur, nxt, prev):
            if kind == "max":
                return nxt if j == 3 else cur
            return prev if kind in ("sums", "out", "mean_y", "var_y") else nxt

        def count(name, b, c, back=0):
            return (b - back + AHEAD) * per[name] + c

        def max_index(q):
            return 1 if q == 3 else q + 2

        def start_ahead(eng, names):
            for name in names:
                eng.sem_inc(s[name], AHEAD * per[name])

        def uses(cur, nxt, prev):
            at = []
            if prev:
                at += [(0, 1, "sums", 0), (0, 2, "sums", 1), (0, 8, "out", 0), (0, 10, "mean_y", 0),
                       (0, 11, "var_y", 0)]
            if nxt:
                at += [(0, 3, "k", 0), (0, 4, "k", 1), (0, 5, "k", 2), (0, 6, "k", 3), (1, 1, "mean_q", 0),
                       (1, 2, "v", 0), (1, 3, "var_q", 0), (1, 4, "v", 1), (1, 5, "v", 2), (1, 7, "v", 3),
                       (1, 9, "q", 0), (3, 8, "max", 3)]
            if cur:
                at += [(q, 8, "max", q) for q in range(3)]
            return sorted(at)

        def rows(eng, iteration):
            def row(b, parity):
                return b, parity
            n0, n1 = len(uses(0, 1, 0)), len(uses(1, 1, 0))
            n2 = len(uses(1, 1, 1))
            iteration(None, row(0, 0), None, 0)
            iteration(row(0, 0), row(1, 1), None, n0)
            with eng.Fori(0, NB // 2 - 1) as i:
                iteration(row(2 * i + 1, 1), row(2 * i + 2, 0), row(2 * i, 0), i * (2 * n2) + (n0 + n1))
                iteration(row(2 * i + 2, 0), row(2 * i + 3, 1), row(2 * i + 1, 1), i * (2 * n2) + (n0 + n1 + n2))
            base = n0 + n1 + (NB - 2) * n2
            iteration(row(NB - 1, 1), None, row(NB - 2, 0), base)
            iteration(None, None, row(NB - 1, 1), base + len(uses(1, 0, 1)))

        def tile_keys(kt):
            return min(P, KEYS - kt * P)

        block = ctx.enter_context(nc.Block())

        @block.sync
        def _(sp):
            start_ahead(sp, dma_per)
            for dst, src in ((w_sb[:, :], ins["x_w"]), (vec[:, :], ins["x_vec"]), (bv[:, :], ins["bv"]),
                             ):
                sp.dma_start(dst, src).then_inc(start_in, 16)

            def load_ctx(b):
                sp.dma_start(ctxT[:, :], ins["ctx"][:, b, :]).then_inc(s["ctx_in"], 16)

            def load_masks(b):
                sp.dma_start(m8[:, :, :], ins["mask_q"][b, :, :].rearrange("(t p) k -> p t k", p=P)
                             ).then_inc(s["m8_in"], 16)
                sp.dma_start(mt8[:, 0:KT - 1, :], ins["mask_k"][b, 0:(KT - 1) * P, :]
                             .rearrange("(t p) q -> p t q", p=P)).then_inc(s["mt8_in"], 16)
                sp.dma_start(mt8[0:KEYS - (KT - 1) * P, KT - 1, :], ins["mask_k"][b, (KT - 1) * P:KEYS, :]
                             ).then_inc(s["mt8_in"], 16)

            def load_k(b, p, q):
                for a in range(3):
                    for c in range(3):
                        r = 24 * a + 8 * c
                        sp.dma_start(k_op[q][r:r + DK, :, :],
                                     k_scr[p, c, 32 * q:32 * q + 32, :].rearrange("(h d) k -> d h k", d=DK)
                                     ).then_inc(kop_in[q], 16)

            load_ctx(0)
            load_masks(0)
            sp.wait_ge(set_pool, N_SETX)
            for i in range(4):
                sp.dma_start(k_op[i][72:75, :, :], onesr[:, :].unsqueeze(1).to_broadcast([3, 4, KEYS])
                             ).then_inc(ones_in, 16)

            def iteration(cur, nxt, prev, base):
                if nxt:
                    b = nxt[0]
                    sp.wait_ge(start_in, 48)
                    sp.wait_ge(s["lcq_ready"], count("lcq_ready", b, 1, back=1))
                    sp.dma_start(xa[:, :], ins["xin"][:, b, :]).then_inc(s["xa_in"], 16)
                if prev:
                    b = prev[0]
                    sp.wait_ge(start_in, 48)
                    sp.wait_ge(s["y1_ready"], count("y1_ready", b, 1, back=1))
                    sp.dma_start(xb[:, :], ins["xin"][:, b, :]).then_inc(s["xb_in"], 16)
                    sp.wait_ge(start_in, 48)
                    sp.wait_ge(s["y1_ready"], count("y1_ready", b, 1))
                    sp.dma_start(x1_scr[:, b, :], y1[:, :]).then_inc(s["x1_kept"], 16)
                    sp.wait_ge(start_in, 48)
                    sp.wait_ge(s["xn_ready"], count("xn_ready", b, 1))
                    sp.dma_start(xn_scr[:, b, :], xn[:, :]).then_inc(s["xn_kept"], 16)
                if nxt:
                    b, p = nxt
                    sp.wait_ge(start_in, 48)
                    sp.wait_ge(s["klo_ready"], count("klo_ready", b, 1))
                    for c in range(3):
                        sp.dma_start(k_scr[p, c], kp[:, c, :]).then_inc(s["kscr_in"], 16)
                    sp.wait_ge(start_in, 48)
                    sp.wait_ge(s["kscr_in"], count("kscr_in", b, 48))
                    sp.wait_ge(start_in, 48)
                    sp.wait_ge(s["e_done"], count("e_done", b, 2 * KT, back=1))
                    load_k(b, p, 0)
                    sp.wait_ge(start_in, 48)
                    sp.wait_ge(s["qlo_ready"], count("qlo_ready", b, 1))
                    for c in range(3):
                        sp.dma_start(q_scr[p, c], qp[:, c, :]).then_inc(s["qscr_in"], 16)
                    sp.wait_ge(start_in, 48)
                    sp.wait_ge(s["qscr_in"], count("qscr_in", b, 48))
                    sp.wait_ge(start_in, 48)
                    sp.wait_ge(s["e_done"], count("e_done", b, 8 * KT, back=2))
                    for a in range(3):
                        for c in range(3):
                            r = 24 * a + 8 * c
                            for op in (q_max, q_exp):
                                sp.dma_start(op[r:r + DK, p, :, :],
                                             q_scr[p, a].rearrange("(h d) q -> d h q", d=DK)
                                             ).then_inc(s["qop_in"], 16)
                    sp.wait_ge(start_in, 48)
                    sp.wait_ge(s["e_done"], count("e_done", b, 4 * KT, back=1))
                    load_k(b, p, 1)
                if nxt:
                    b, p = nxt
                    sp.wait_ge(start_in, 48)
                    sp.wait_ge(s["vx_ready"], count("vx_ready", b, 4))
                    load_ctx(b + 1)
                    sp.wait_ge(start_in, 48)
                    sp.wait_ge(s["mq_ready"], count("mq_ready", b, 1))
                    sp.wait_ge(s["mk_ready"], count("mk_ready", b, 1))
                    load_masks(b + 1)
                if nxt:
                    b, p = nxt
                    for q in (2, 3):
                        sp.wait_ge(start_in, 48)
                        sp.wait_ge(s["e_done"], count("e_done", b, 2 * KT * (q + 1), back=1))
                        load_k(b, p, q)

            rows(sp, iteration)
            sp.wait_ge(s["ctx_in"], count("ctx_in", NB, 16))
            sp.wait_ge(s["x1_kept"], count("x1_kept", NB, 0))
            sp.wait_ge(s["xn_kept"], count("xn_kept", NB, 0))
            sp.wait_ge(s["m8_in"], count("m8_in", NB, 16))
            sp.wait_ge(s["mt8_in"], count("mt8_in", NB, 32))

        @block.gpsimd
        def _(pool):
            start_ahead(pool, pool_own)
            for i in range(4):
                nc.gpsimd.memset(k_op[i][:, :, :], 0.0).then_inc(set_pool, 1)
            nc.gpsimd.memset(q_max[:, :, :, :], 0.0).then_inc(set_pool, 1)
            nc.gpsimd.memset(q_exp[:, :, :, :], 0.0).then_inc(set_pool, 1)
            nc.gpsimd.memset(onesr[:, :], 1.0).then_inc(set_pool, 1)
            nc.gpsimd.memset(vx[:, :, :, :, :], 1.0).then_inc(set_pool, 1)

            def iteration(cur, nxt, prev, base):
                if nxt:
                    b, p = nxt
                    pool.wait_ge(s["m8_in"], count("m8_in", b, 16))
                    wait_apart(pool, pool_passed, s["s_max"], count("s_max", b, 64, back=2))
                    nc.gpsimd.tensor_scalar(mq[:, p, :, :], m8[:, :, :], -BIG, 1.0, ALU.mult, ALU.mult
                                            ).then_inc(s["mq_ready"], 1)
                    pool.wait_ge(s["mt8_in"], count("mt8_in", b, 32))
                    wait_apart(pool, pool_passed, s["e_done"], count("e_done", b, 8 * KT, back=2))
                    nc.gpsimd.tensor_scalar(mk[:, p, 0:KT - 1, :], mt8[:, 0:KT - 1, :], -BIG, 1.0, ALU.mult, ALU.mult)
                    r = KEYS - (KT - 1) * P
                    nc.gpsimd.tensor_scalar(mk[0:r, p, KT - 1, :], mt8[0:r, KT - 1, :], -BIG, 1.0, ALU.mult, ALU.mult
                                            ).then_inc(s["mk_ready"], 1)
            rows(pool, iteration)

        @block.scalar
        def _(act):
            start_ahead(act, act_own)
            act.wait_ge(start_in, 48)
            nc.scalar.activation(gate_x[:, :], vec[:, XV_G:XV_G + 1], ACT.Tanh).then_inc(gate_ready, 1)
            load_tables(nc, act, EXP_LN_TABLES)

            def rstd(kind, row, i):
                b, _ = row
                act.wait_ge(s[f"lve{kind}_ready"], count(f"lve{kind}_ready", b, 1))
                act.wait_ge(s[f"lrs{kind}_ready"], count(f"lrs{kind}_ready", b, 1, back=1))
                nc.scalar.activation(lln[:, i, :], lve[:, i, :], ACT.Ln).then_inc(s[f"lln{kind}_ready"], 1)
                act.wait_ge(s[f"lln{kind}_ready"], count(f"lln{kind}_ready", b, 1))
                done = "xq_ready" if kind == "q" else "xn_ready"
                act.wait_ge(s[done], count(done, b, 1, back=1))
                nc.scalar.activation(lrs[:, i, :], lln[:, i, :], ACT.Exp, scale=-0.5
                                     ).then_inc(s[f"lrs{kind}_ready"], 1)

            def iteration(cur, nxt, prev, base):
                where = uses(cur, nxt, prev)
                for q in range(4):
                    for kt in range(KT):
                        if cur:
                            b, p = cur
                            n = tile_keys(kt)
                            g = q * KT + kt
                            for i in range(2):
                                act.wait_ge(s["e_done"], count("e_done", b, 2 * g + i + 1))
                                act.wait_ge(s["pv_done"], count("pv_done", b, g - 1))
                                nc.scalar.activation(eT[0:n, g % 2, i * 512:(i + 1) * 512], b_e[i][0:n, :],
                                                     ACT.Exp).then_inc(s["e_ready"], 1)
                        at = (q, kt)
                        for i, (*when, kind, j) in enumerate(where):
                            if tuple(when) == at and kind == "k":
                                b = nxt[0]
                                n = min(512, KEYS - 512 * j)
                                act.wait_ge(bank_filled, base + i + 1)
                                act.wait_ge(s["klo_ready"], count("klo_ready", b, 1, back=1))
                                nc.scalar.activation(kf[:, 512 * j:512 * j + n], b_p[:, 0:n], ACT.Identity,
                                                     bias=vec[:, XV_BK:XV_BK + 1]).then_inc(s["kf_ready"], 1)
                        if nxt and at == (0, 10):
                            b = nxt[0]
                            act.wait_ge(s["kf_ready"], count("kf_ready", b, 4))
                            act.wait_ge(s["kscr_in"], count("kscr_in", b, 48, back=1))
                            nc.scalar.activation(kp[:, 0, :], kf[:, :], ACT.Copy).then_inc(s["khi_ready"], 1)
                        if nxt and at == (0, 11):
                            b = nxt[0]
                            act.wait_ge(s["kres_ready"], count("kres_ready", b, 1))
                            nc.scalar.activation(kp[:, 1, :], kf[:, :], ACT.Copy).then_inc(s["kmid_ready"], 1)
                        if nxt and at == (1, 10):
                            b = nxt[0]
                            act.wait_ge(s["qf_ready"], count("qf_ready", b, 1))
                            act.wait_ge(s["qscr_in"], count("qscr_in", b, 48, back=1))
                            nc.scalar.activation(qp[:, 0, :], qf[:, :], ACT.Copy).then_inc(s["qhi_ready"], 1)
                        if nxt and at == (1, 11):
                            b = nxt[0]
                            act.wait_ge(s["qres_ready"], count("qres_ready", b, 1))
                            nc.scalar.activation(qp[:, 1, :], qf[:, :], ACT.Copy).then_inc(s["qmid_ready"], 1)
                        if nxt and at == (1, 4):
                            rstd("q", nxt, 0)
                        if prev and at == (0, 12):
                            rstd("y", prev, 1)
                        if kt == 10:
                            item = (cur, q + 1) if q < 3 else (nxt, 0)
                            if item[0]:
                                (b, p), sq = item
                                m = max_index(q)
                                bm = b
                                act.wait_ge(s["mp_ready"], count("mp_ready", bm, m))
                                act.wait_ge(s["e_done"], count("e_done", bm, 8 * KT, back=2))
                                for c in range(3):
                                    act.dma_start(q_exp[72 + c:73 + c, p, 4 * sq:4 * sq + 4, :], mp[:, c, :]
                                                  ).then_inc(s["mrow_in"], 16)
            rows(act, iteration)

        @block.vector
        def _(dve):
            mine = [n for n in per if n not in pe_own + act_own + pool_own and n not in dma_per]
            start_ahead(dve, mine)
            nc.vector.memset(b_pv[:, :], 0.0).then_inc(set_dve, 1)
            dve.wait_ge(start_in, 48)
            dve.wait_ge(set_pool, N_SETX)
            dve.wait_ge(gate_ready, 1)

            def iteration(cur, nxt, prev, base):
                where = uses(cur, nxt, prev)

                def s_units(row, sq, kt):
                    b, p = row
                    if kt == 0:
                        dve.wait_ge(s["mq_ready"], count("mq_ready", b, 1))
                        dve.wait_ge(s["mx_ready"], count("mx_ready", b, sq))
                    for u in S_UNITS[kt]:
                        qt, h, half = u // 8, (u // 2) % 4, u % 2
                        n = 1024 if half == 0 else KEYS - 1024
                        dve.wait_ge(s["s_done"], count("s_done", b, 16 * sq + u + 1))
                        wait_apart(dve, dve_passed, s["s_max"], count("s_max", b, 16 * sq + u - 1))
                        nc.vector.tensor_tensor_reduce(
                            junk[:, half, 0:n], b_s[u % 2][:, 0:n], mq[:, p, qt, half * 1024:half * 1024 + n],
                            1.0, LOWEST, ALU.add, ALU.max, smax[:, half, 4 * qt + h:4 * qt + h + 1]
                        ).then_inc(s["s_max"], 1)

                def bank(i, kind, j):
                    dve.wait_ge(bank_filled, base + i + 1)
                    if kind == "max":
                        row = nxt if j == 3 else cur
                        b = row[0]
                        m = max_index(j)
                        dve.wait_ge(s["mres2_ready"], count("mres2_ready", b, m - 1))
                        nc.vector.tensor_scalar(mneg[:, :], b_p[0:4, 0:S], -1.0, None, ALU.mult
                                                ).then_inc(s["mneg_ready"], 1)
                        dve.wait_ge(s["mneg_ready"], count("mneg_ready", b, m))
                        dve.wait_ge(s["mrow_in"], count("mrow_in", b, 48 * (m - 1)))
                        nc.vector.tensor_copy(mp[:, 0, :], mneg[:, :]).then_inc(s["mhi_ready"], 1)
                        dve.wait_ge(s["mhi_ready"], count("mhi_ready", b, m))
                        nc.vector.tensor_tensor(mres[:, :], mneg[:, :], mp[:, 0, :], ALU.subtract
                                                ).then_inc(s["mres_ready"], 1)
                        dve.wait_ge(s["mres_ready"], count("mres_ready", b, m))
                        nc.vector.tensor_copy(mp[:, 1, :], mres[:, :]).then_inc(s["mmid_ready"], 1)
                        dve.wait_ge(s["mmid_ready"], count("mmid_ready", b, m))
                        nc.vector.tensor_tensor(mres2[:, :], mres[:, :], mp[:, 1, :], ALU.subtract
                                                ).then_inc(s["mres2_ready"], 1)
                        dve.wait_ge(s["mres2_ready"], count("mres2_ready", b, m))
                        nc.vector.tensor_copy(mp[:, 2, :], mres2[:, :]).then_inc(s["mp_ready"], 1)
                    elif kind == "v":
                        b, p = nxt
                        nt = 4 if j < 3 else 1
                        n = P if j < 3 else tile_keys(KT - 1)
                        dve.wait_ge(s["pv_done"], count("pv_done", b, 4 * KT, back=2))
                        for t in range(nt):
                            ins_ = nc.vector.tensor_tensor(
                                vx[0:n, p, 4 * j + t, :, 0:DK],
                                b_p[0:n, t * P:(t + 1) * P].rearrange("p (h d) -> p h d", d=DK),
                                bv[0:n, :].rearrange("p (h d) -> p h d", d=DK), ALU.add)
                        ins_.then_inc(s["vx_ready"], 1)
                    elif kind == "q":
                        b = nxt[0]
                        dve.wait_ge(s["qlo_ready"], count("qlo_ready", b, 1, back=1))
                        nc.vector.tensor_scalar(qf[:, :], b_p[:, 0:S], vec[:, XV_BQ:XV_BQ + 1], DK ** -0.5,
                                                ALU.add, ALU.mult).then_inc(s["qf_ready"], 1)
                    elif kind in ("mean_q", "mean_y"):
                        c, row, i_ = ("q", nxt, 0) if kind == "mean_q" else ("y", prev, 1)
                        b = row[0]
                        src = xa[:, :] if c == "q" else y1[:, :]
                        done = "xq_ready" if c == "q" else "xn_ready"
                        dve.wait_ge(s[done], count(done, b, 1, back=1))
                        if c == "q":
                            dve.wait_ge(s["xa_in"], count("xa_in", b, 16))
                        nc.vector.tensor_tensor(lc[:, i_, :], src, b_p[:, 0:S], ALU.subtract
                                                ).then_inc(s[f"lc{c}_ready"], 1)
                        dve.wait_ge(s[f"lc{c}_ready"], count(f"lc{c}_ready", b, 1))
                        dve.wait_ge(s[f"lve{c}_ready"], count(f"lve{c}_ready", b, 1, back=1))
                        nc.vector.tensor_tensor(lsq[:, i_, :], lc[:, i_, :], lc[:, i_, :], ALU.mult
                                                ).then_inc(s[f"lsq{c}_ready"], 1)
                    elif kind in ("var_q", "var_y"):
                        c, row, i_ = ("q", nxt, 0) if kind == "var_q" else ("y", prev, 1)
                        b = row[0]
                        dve.wait_ge(s[f"lln{c}_ready"], count(f"lln{c}_ready", b, 1, back=1))
                        nc.vector.tensor_scalar(lve[:, i_, :], b_p[:, 0:S], 1e-5, None, ALU.add
                                                ).then_inc(s[f"lve{c}_ready"], 1)
                    elif kind == "sums":
                        b = prev[0]
                        dve.wait_ge(s["un_ready"], count("un_ready", b, j + 1, back=1))
                        nc.vector.tensor_copy(ru[:, 2 * j:2 * j + 2, :], b_p[:, :].rearrange("p (q t) -> p q t", q=2)
                                              ).then_inc(s["sums_kept"], 1)
                    elif kind == "out":
                        b = prev[0]
                        dve.wait_ge(s["y1_ready"], count("y1_ready", b, 1, back=1))
                        nc.vector.tensor_scalar(t1[:, :], b_p[:, 0:S], vec[:, XV_BO:XV_BO + 1], gate_x[:, 0:1],
                                                ALU.add, ALU.mult).then_inc(s["t1_ready"], 1)
                    if kind == "out":
                        b = prev[0]
                        dve.wait_ge(s["t1_ready"], count("t1_ready", b, 1))
                        dve.wait_ge(s["x1_kept"], count("x1_kept", b, 16, back=1))
                        dve.wait_ge(s["xb_in"], count("xb_in", b, 16))
                        dve.wait_ge(s["lcy_ready"], count("lcy_ready", b, 1, back=1))
                        nc.vector.tensor_tensor(y1[:, :], t1[:, :], xb[:, :], ALU.add
                                                ).then_inc(s["y1_ready"], 1)

                for q in range(4):
                    for kt in range(KT):
                        item = (cur, q + 1) if q < 3 else (nxt, 0)
                        if item[0] and kt < len(S_UNITS):
                            s_units(item[0], item[1], kt)
                        if prev and q == 0 and 3 <= kt <= 6:
                            b = prev[0]
                            dve.wait_ge(s["sums_kept"], count("sums_kept", b, 2))
                            nc.vector.reciprocal(ru[:, kt - 3, :], ru[:, kt - 3, :]).then_inc(s["ru_ready"], 1)
                        if prev and q == 0 and kt in (5, 7):
                            j = (kt - 5) // 2
                            b = prev[0]
                            dve.wait_ge(s["ru_ready"], count("ru_ready", b, 2 * j + 2))
                            nc.vector.tensor_tensor(ru[:, 2 * j:2 * j + 2, :], u4[:, 2 * j:2 * j + 2, :],
                                                    ru[:, 2 * j:2 * j + 2, :], ALU.mult).then_inc(s["un_ready"], 1)
                        if cur and kt == 0 and q > 0:
                            keep_u(dve, cur, q - 1)
                        if item[0] and kt == 8:
                            b = item[0][0]
                            m = max_index(q)
                            dve.wait_ge(s["s_max"], count("s_max", b, 16 * item[1] + 16))
                            dve.wait_ge(s["mneg_ready"], count("mneg_ready", b, m - 1))
                            nc.vector.tensor_tensor(smax1[:, :], smax[:, 0, :], smax[:, 1, :], ALU.max
                                                    ).then_inc(s["mx_ready"], 1)
                        for i, (uq, ukt, kind, j) in enumerate(where):
                            if (uq, ukt) == (q, kt) and kind != "k":
                                bank(i, kind, j)
                        at = (q, kt)
                        if nxt and at == (0, 10):
                            b = nxt[0]
                            dve.wait_ge(s["khi_ready"], count("khi_ready", b, 1))
                            nc.vector.tensor_tensor(kf[:, :], kf[:, :], kp[:, 0, :], ALU.subtract
                                                    ).then_inc(s["kres_ready"], 1)
                        if nxt and at == (0, 12):
                            b = nxt[0]
                            dve.wait_ge(s["kmid_ready"], count("kmid_ready", b, 1))
                            nc.vector.tensor_tensor(kp[:, 2, :], kf[:, :], kp[:, 1, :], ALU.subtract
                                                    ).then_inc(s["klo_ready"], 1)
                        if nxt and at == (1, 10):
                            b = nxt[0]
                            dve.wait_ge(s["qhi_ready"], count("qhi_ready", b, 1))
                            nc.vector.tensor_tensor(qf[:, :], qf[:, :], qp[:, 0, :], ALU.subtract
                                                    ).then_inc(s["qres_ready"], 1)
                        if nxt and at == (1, 11):
                            b = nxt[0]
                            dve.wait_ge(s["qmid_ready"], count("qmid_ready", b, 1))
                            nc.vector.tensor_tensor(qp[:, 2, :], qf[:, :], qp[:, 1, :], ALU.subtract
                                                    ).then_inc(s["qlo_ready"], 1)
                        if nxt and at == (1, 6):
                            b = nxt[0]
                            dve.wait_ge(s["lrsq_ready"], count("lrsq_ready", b, 1))
                            nc.vector.tensor_tensor(xq[:, :], lc[:, 0, :], lrs[:, 0, :], ALU.mult
                                                    ).then_inc(s["xq_ready"], 1)
                        if prev and at == (1, 1):
                            b = prev[0]
                            dve.wait_ge(s["lrsy_ready"], count("lrsy_ready", b, 1))
                            dve.wait_ge(s["xn_kept"], count("xn_kept", b, 16, back=1))
                            nc.vector.tensor_tensor(xn[:, :], lc[:, 1, :], lrs[:, 1, :], ALU.mult
                                                    ).then_inc(s["xn_ready"], 1)
                if cur:
                    keep_u(dve, cur, 3)

            def keep_u(dve, row, q):
                b = row[0]
                dve.wait_ge(s["pv_done"], count("pv_done", b, (q + 1) * KT))
                dve.wait_ge(s["un_ready"], count("un_ready", b, 2, back=1))
                nc.vector.tensor_copy(u4[:, q, :], b_pv[:, 0:S]).then_inc(s["u_kept"], 1)
            rows(dve, iteration)

        @block.tensor
        def _(pe):
            start_ahead(pe, pe_own)
            pe.wait_ge(start_in, 48)
            pe.wait_ge(set_pool, N_SETX)
            pe.wait_ge(set_dve, 1)
            pe.wait_ge(ones_in, 64)

            def iteration(cur, nxt, prev, base):
                where = uses(cur, nxt, prev)

                def products(q, kt):
                    b, p = cur
                    n = tile_keys(kt)
                    g = q * KT + kt
                    pe.wait_ge(s["e_ready"], count("e_ready", b, 2 * g + 2))
                    if kt == 0:
                        pe.wait_ge(s["vx_ready"], count("vx_ready", b, 4))
                        pe.wait_ge(s["u_kept"], count("u_kept", b, q))
                    for h in range(4):
                        last = nc.tensor.matmul(b_pv[32 * h:32 * h + DK + 1, 0:S], vx[0:n, p, kt, 4 * q + h, :],
                                                eT[0:n, g % 2, h * S:(h + 1) * S],
                                                start=(kt == 0), stop=(kt == KT - 1), tile_position=(0, 32 * h))
                    last.then_inc(s["pv_done"], 1)

                def bank(i, kind, j):
                    if i:
                        _, _, kind0, j0 = where[i - 1]
                        pe.wait_ge(*last_reader(kind0, j0, row_of(kind0, j0, cur, nxt, prev)))
                    elif cur:
                        pe.wait_ge(*last_reader("max", 3, cur))
                    elif prev:
                        pe.wait_ge(*last_reader("max", 2, prev))
                    if kind == "max":
                        row = nxt if j == 3 else cur
                        b = row[0]
                        pe.wait_ge(s["mx_ready"], count("mx_ready", b, max_index(j)))
                        for qt in range(2):
                            last = nc.tensor.transpose(b_p[0:4, qt * P:(qt + 1) * P], smax1[:, 4 * qt:4 * qt + 4],
                                                       ident[:, :])
                    elif kind == "k":
                        b = nxt[0]
                        n = min(512, KEYS - 512 * j)
                        pe.wait_ge(s["ctx_in"], count("ctx_in", b, 16))
                        last = nc.tensor.matmul(b_p[:, 0:n], w_sb[:, XW_K:XW_K + P], ctxT[:, 512 * j:512 * j + n],
                                                start=True, stop=True)
                    elif kind == "v":
                        nt = 4 if j < 3 else 1
                        for t in range(nt):
                            k0 = (4 * j + t) * P
                            n = min(P, KEYS - k0)
                            last = nc.tensor.matmul(b_p[0:n, t * P:(t + 1) * P], ctxT[:, k0:k0 + n],
                                                    w_sb[:, XW_V:XW_V + P], start=True, stop=True)
                    elif kind == "q":
                        b = nxt[0]
                        pe.wait_ge(s["xq_ready"], count("xq_ready", b, 1))
                        last = nc.tensor.matmul(b_p[:, 0:S], w_sb[:, XW_Q:XW_Q + P], xq[:, :], start=True, stop=True)
                    elif kind == "mean_q":
                        b = nxt[0]
                        pe.wait_ge(s["xa_in"], count("xa_in", b, 16))
                        last = nc.tensor.matmul(b_p[:, 0:S], w_sb[:, XW_M:XW_M + P], xa[:, :],
                                                start=True, stop=True)
                    elif kind == "mean_y":
                        b = prev[0]
                        pe.wait_ge(s["y1_ready"], count("y1_ready", b, 1))
                        last = nc.tensor.matmul(b_p[:, 0:S], w_sb[:, XW_M:XW_M + P], y1[:, :], start=True, stop=True)
                    elif kind in ("var_q", "var_y"):
                        c, row, i_ = ("q", nxt, 0) if kind == "var_q" else ("y", prev, 1)
                        pe.wait_ge(s[f"lsq{c}_ready"], count(f"lsq{c}_ready", row[0], 1))
                        last = nc.tensor.matmul(b_p[:, 0:S], w_sb[:, XW_M:XW_M + P], lsq[:, i_, :],
                                                start=True, stop=True)
                    elif kind == "sums":
                        b = prev[0]
                        pe.wait_ge(s["u_kept"], count("u_kept", b, 4))
                        last = nc.tensor.matmul(b_p[:, :], w_sb[:, XW_S:XW_S + P], u4[:, 2 * j:2 * j + 2, :],
                                                start=True, stop=True)
                    elif kind == "out":
                        b = prev[0]
                        pe.wait_ge(s["un_ready"], count("un_ready", b, 2))
                        for q in range(4):
                            last = nc.tensor.matmul(b_p[:, 0:S], w_sb[:, XW_O + q * P:XW_O + (q + 1) * P], ru[:, q, :],
                                                    start=(q == 0), stop=(q == 3))
                    last.then_inc(bank_filled, 1)

                for q in range(4):
                    for kt in range(KT):
                        item = (cur, q + 1) if q < 3 else (nxt, 0)
                        if item[0] and kt < len(S_UNITS):
                            (b, p), sq = item
                            if kt == 0:
                                pe.wait_ge(kop_in[sq], b * KOP + KOP)
                                pe.wait_ge(s["qop_in"], count("qop_in", b, 18 * 16))
                            for u in S_UNITS[kt]:
                                qt, h, half = u // 8, (u // 2) % 4, u % 2
                                pe.wait_ge(s["s_max"], count("s_max", b, 16 * sq + u - 1))
                                for c in range(2):
                                    k0 = half * 1024 + c * 512
                                    n = min(512, KEYS - k0)
                                    last = nc.tensor.matmul(b_s[u % 2][:, c * 512:c * 512 + n],
                                                            q_max[:, p, 4 * sq + h, qt * P:(qt + 1) * P],
                                                            k_op[sq][:, h, k0:k0 + n], start=True, stop=True)
                                last.then_inc(s["s_done"], 1)
                        if cur:
                            b, p = cur
                            n = tile_keys(kt)
                            g = q * KT + kt
                            if kt == 0:
                                pe.wait_ge(s["mk_ready"], count("mk_ready", b, 1))
                                pe.wait_ge(s["mrow_in"], count("mrow_in", b, 48 * (q + 1)))
                            for i in range(2):
                                pe.wait_ge(s["e_ready"], count("e_ready", b, 2 * g + i - 1))
                                nc.tensor.matmul(b_e[i][0:n, :], identb[0:n, 0:n],
                                                 mk[0:n, p, kt, :].unsqueeze(1).to_broadcast([n, 2, S]),
                                                 start=True, stop=False, skip_group_check=True)
                                for j in range(2):
                                    last = nc.tensor.matmul(
                                        b_e[i][0:n, j * S:(j + 1) * S], k_op[q][:, 2 * i + j, kt * P:kt * P + n],
                                        q_exp[:, p, 4 * q + 2 * i + j, :], start=False, stop=True,
                                        skip_group_check=True)
                                last.then_inc(s["e_done"], 1)
                            if g:
                                products(*divmod(g - 1, KT))
                        for i, (uq, ukt, kind, j) in enumerate(where):
                            if (uq, ukt) == (q, kt):
                                bank(i, kind, j)
                if cur:
                    products(3, KT - 1)
            rows(pe, iteration)


def ffn_phase(nc, xn_scr, x1_scr, ident, identb, ins, out, NB, DEPTH):
    with ExitStack() as ctx:
        def sb(name, shape, dt=F32):
            return ctx.enter_context(nc.sbuf_tensor(name, shape, dt))

        def bank(name):
            return ctx.enter_context(nc.psum_tensor(name, [P, 512], F32))

        xT = sb("xT", [P, NB, S])
        xres = sb("xres", [P, NB, S])
        eps_c = sb("eps_c", [P, 3])
        weights = sb("weights", [P, W_END])
        par = sb("par", [P, N_PAR])
        par_a = sb("par_a", [P, P_G])
        rot_raw = sb("rot_raw", [P, 4, S])
        rot_tab = sb("rot_tab", [P, 4, S])
        lmask_f = sb("lmask_f", [P, 2 * KW])
        lmask = sb("lmask", [P, 2, GMAX, KW], BF16)
        pair_ones = sb("pair_ones", [P, P])
        mean_mat = sb("mean_mat", [P, P])
        gate = sb("gate", [P, 1])
        gate_t = sb("gate_t", [P, 1])
        xs = sb("xs", [P, 2, S])
        qT = sb("qT", [P, 2, NJ, S])
        kT = sb("kT", [P, 2, 2, NJ, WIN + S])
        v = sb("v", [P, 2, 2, INNER])
        sq = sb("sq", [P, 2, 2 * S])
        ln_n2 = sb("ln_n2", [P, 2 * S])
        rnorm = sb("rnorm", [P, 2, 2 * S])
        rot_c = sb("rot_c", [P, 2, 2 * S])
        rot_s = sb("rot_s", [P, 2, 2 * S])
        probs = sb("probs", [P, 2, 2, PAD + GMAX * KW])
        nmax = sb("nmax", [P, 2, GMAX])
        psums = sb("psums", [P, 2, 2, GMAX])
        rsums = sb("rsums", [P, 2, 2, GMAX])
        probsT = sb("probsT", [P, 2, GMAX * KW])
        oT = sb("oT", [P, NJ, S])
        x1 = sb("x1", [P, S])
        xs1 = sb("xs1", [P, S])
        xc = sb("xc", [P, S])
        xsq = sb("xsq", [P, S])
        ln_v = sb("ln_v", [P, S])
        rstd = sb("rstd", [P, S])
        xn = sb("xn", [P, S])
        xg = sb("xg", [P, S])
        gt = sb("gt", [P, FB * S])
        at = sb("at", [P, FB * S])
        gg = sb("gg", [P, FB * S])
        hT = sb("hT", [P, FB * S])

        b_qk0, b_qk1, b_nv, b_even, b_odd, b_pt, b_o, b_c = (bank(n) for n in (
            "b_qk0", "b_qk1", "b_nv", "b_even", "b_odd", "b_pt", "b_o", "b_c"))
        b_sc = [b_even, b_odd]
        b_qk = [b_qk0, b_qk1]

        per = dict(xs_ready=2, qk_done=STEPS, shuf_ready=STEPS, v_done=4, v_kept=4, sq_ready=STEPS, norm_done=STEPS,
                   ln_ready=STEPS, rnorm_ready=STEPS, rotc_ready=STEPS, rots_ready=STEPS, sum_ready=STEPS,
                   rot_ready=STEPS, scores_done=12, max_ready=12, exp_ready=12, rsum_ready=12, pn_ready=12,
                   pt_done=12, pt_kept=12, o_done=6, o_kept=6, wo_done=1, x1_ready=1, xs1_ready=2, mu_done=1,
                   xc_ready=1, xsq_ready=1, var_done=1, lnv_ready=1, rstd_ready=1, xn_ready=1, xg_ready=1,
                   h_done=3, h_kept=6, gelu_ready=1, hh_ready=1, w2_done=1, x_ready=1)
        owner = dict(xs_ready="pool", qk_done="pe", shuf_ready="dve", v_done="pe", v_kept="act", sq_ready="act", norm_done="pe",
                     ln_ready="act", rnorm_ready="act", rotc_ready="dve", rots_ready="dve", sum_ready="dve",
                     rot_ready="dve", scores_done="pe", max_ready="dve", exp_ready="act", rsum_ready="dve",
                     pn_ready="pool", pt_done="pe", pt_kept="act", o_done="pe", o_kept="dve", wo_done="pe",
                     x1_ready="dve", xs1_ready="pool", mu_done="pe", xc_ready="dve", xsq_ready="dve",
                     var_done="pe", lnv_ready="act", rstd_ready="act", xn_ready="dve", xg_ready="dve",
                     h_done="pe", h_kept="dve", gelu_ready="act", hh_ready="dve", w2_done="pe", x_ready="dve")
        sems = {n: ctx.enter_context(nc.semaphore(n)) for n in per}
        dve_passed = ctx.enter_context(nc.semaphore("dve_passed"))
        sp_passed = ctx.enter_context(nc.semaphore("sp_passed"))
        pool_passed = ctx.enter_context(nc.semaphore("pool_passed"))
        part_in = [ctx.enter_context(nc.semaphore(f"part_in{i}")) for i in range(len(W_PARTS))]
        scales_in = ctx.enter_context(nc.semaphore("scales_in"))
        vectors_in = ctx.enter_context(nc.semaphore("vectors_in"))
        consts_in = ctx.enter_context(nc.semaphore("consts_in"))
        setup = ctx.enter_context(nc.semaphore("setup"))
        setup2 = ctx.enter_context(nc.semaphore("setup2"))
        tab_ready = ctx.enter_context(nc.semaphore("tab_ready"))
        gate_ready = ctx.enter_context(nc.semaphore("gate_ready"))
        fin_ready = ctx.enter_context(nc.semaphore("fin_ready"))
        out_sent = ctx.enter_context(nc.semaphore("out_sent"))

        def count(name, n, c, back=0):
            return n * per[name] + (AHEAD - back) * per[name] + c

        def start_ahead(eng, who):
            for name in per:
                if owner[name] == who:
                    eng.sem_inc(sems[name], AHEAD * per[name])

        def rows(eng, layer_start, iteration):
            def row(layer, b, parity):
                return layer * NB + b, b, parity, layer * 16 + 16

            def whole_layer(layer, before):
                iteration(row(layer, 2, 0), row(layer, 1, 1), row(layer, 0, 0), before)
                iteration(row(layer, 3, 1), row(layer, 2, 0), row(layer, 1, 1), row(layer, 0, 0))
                with eng.Fori(1, NB // 2 - 1) as i:
                    b = 2 * i
                    iteration(row(layer, b + 2, 0), row(layer, b + 1, 1), row(layer, b, 0), row(layer, b - 1, 1))
                    iteration(row(layer, b + 3, 1), row(layer, b + 2, 0), row(layer, b + 1, 1), row(layer, b, 0))

            layer_start(0)
            iteration(row(0, 0, 0), None, None, None)
            iteration(row(0, 1, 1), row(0, 0, 0), None, None)
            whole_layer(0, None)
            last = [(NB - 3, 1), (NB - 2, 0), (NB - 1, 1)]
            with eng.Fori(1, DEPTH) as layer:
                layer_start(layer)
                d, c, b = (row(layer - 1, *x) for x in last)
                iteration(row(layer, 0, 0), b, c, d)
                iteration(row(layer, 1, 1), row(layer, 0, 0), b, c)
                whole_layer(layer, b)
            d, c, b = (row(DEPTH - 1, *x) for x in last)
            iteration(None, b, c, d)
            iteration(None, None, b, c)
            iteration(None, None, None, b)

        block = ctx.enter_context(nc.Block())

        @block.sync
        def _(sp):
            lm = ins["lmask"]
            for dst, src in ((xT[:, :, :], xn_scr), (xres[:, :, :], x1_scr), (rot_raw[:, :, :], ins["rot"]),
                             (lmask_f[:, :], lm[:, 0:2 * KW]), (pair_ones[:, :], lm[:, 2 * KW:2 * KW + P]),
                             (mean_mat[:, :], lm[:, 2 * KW + P:]), (gate[:, :], ins["gate_f"])):
                sp.dma_start(dst, src).then_inc(consts_in, 16)

            def load(part, layer):
                c0, c1 = W_PARTS[part]
                sp.dma_start(weights[:, c0:c1], ins["ffn_w"][layer, :, c0:c1]).then_inc(part_in[part], 16)

            def load_scales(layer):
                sp.dma_start(par_a[:, :], ins["ffn_vec"][layer, :, 0:P_G]).then_inc(scales_in, 16)

            def load_vectors(layer):
                sp.dma_start(par[:, :], ins["ffn_vec"][layer, :, :]).then_inc(vectors_in, 16)

            load_scales(0)
            for part in (PART_V, PART_Q, PART_K, PART_O, PART_1, PART_2):
                load(part, 0)
            load_vectors(0)
            with sp.Fori(1, DEPTH) as layer:
                last = layer * NB - 1
                wait_apart(sp, sp_passed, sems["v_done"], count("v_done", last, 4))
                load_scales(layer)
                load(PART_V, layer)
                wait_apart(sp, sp_passed, sems["qk_done"], count("qk_done", last, STEPS // 2))
                load(PART_Q, layer)
                wait_apart(sp, sp_passed, sems["qk_done"], count("qk_done", last, STEPS))
                load(PART_K, layer)
                wait_apart(sp, sp_passed, sems["wo_done"], count("wo_done", last, 1))
                load(PART_O, layer)
                wait_apart(sp, sp_passed, sems["h_done"], count("h_done", last, 3))
                load(PART_1, layer)
                wait_apart(sp, sp_passed, sems["x_ready"], count("x_ready", last, 1))
                load(PART_2, layer)
                load_vectors(layer)
            sp.wait_ge(fin_ready, NB)
            sp.dma_start(out, xT[:, :, :]).then_inc(out_sent, 16)
            sp.wait_ge(out_sent, 16)

        @block.gpsimd
        def _(pool):
            s = sems
            start_ahead(pool, "pool")
            nc.gpsimd.memset(xs[:, :, :], 0.0).then_inc(setup, 1)
            nc.gpsimd.memset(xs1[:, :], 0.0).then_inc(setup, 1)
            for i, value in enumerate((1e-5, 2.0 ** -64, 10.0 * float(np.log(2.0)))):
                nc.gpsimd.memset(eps_c[:, i:i + 1], value).then_inc(setup, 1)
            nc.gpsimd.memset(kT[:, :, :, :, :], 0.0).then_inc(setup, 1)
            nc.gpsimd.memset(probs[:, :, :, :], 0.0).then_inc(setup, 1)
            pool.wait_ge(setup, 7)
            pool.wait_ge(consts_in, 16 * 7)

            def layer_start(layer):
                pool.wait_ge(scales_in, 16 * layer + 16)
                wait_apart(pool, pool_passed, s["rots_ready"], count("rots_ready", layer * NB, 0))
                for i, col in enumerate((P_Q, P_QR, P_K, P_KR)):
                    nc.gpsimd.tensor_scalar(rot_tab[:, i, :], rot_raw[:, i, :], par_a[:, col:col + 1], 1.0,
                                            ALU.mult, ALU.mult).then_inc(tab_ready, 1)

            def iteration(A, B, C, D):
                if A:
                    n, b, p, loaded = A
                    if not isinstance(loaded, int):
                        pool.wait_ge(s["x_ready"], count("x_ready", n, 1, back=NB))
                    pool.wait_ge(s["v_done"], count("v_done", n, 4, back=2))
                    wait_apart(pool, pool_passed, s["qk_done"], count("qk_done", n, STEPS, back=2))
                    nc.gpsimd.tensor_copy(xs[0:DH, p, :], xT[0:DH, b, :]).then_inc(s["xs_ready"], 1)
                    wait_apart(pool, pool_passed, s["xs_ready"], count("xs_ready", n, 1))
                    nc.gpsimd.tensor_copy(xs[DH:P, p, 1:S], xT[DH:P, b, 0:S - 1]).then_inc(s["xs_ready"], 1)
                    pool.wait_ge(s["xs_ready"], count("xs_ready", n, 2))
                for k in range(STEPS):
                    if C and k == 2:
                        n = C[0]
                        pool.wait_ge(s["x1_ready"], count("x1_ready", n, 1))
                        wait_apart(pool, pool_passed, s["xc_ready"], count("xc_ready", n, 1, back=1))
                        nc.gpsimd.tensor_copy(xs1[0:DH, :], x1[0:DH, :]).then_inc(s["xs1_ready"], 1)
                        wait_apart(pool, pool_passed, s["xs1_ready"], count("xs1_ready", n, 1))
                        nc.gpsimd.tensor_copy(xs1[DH:P, 1:S], x1[DH:P, 0:S - 1]).then_inc(s["xs1_ready"], 1)
                        pool.wait_ge(s["xs1_ready"], count("xs1_ready", n, 2))
                    if B and k < len(GROUPS):
                        n, gn = B[0], GROUPS[k][2]
                        for e in range(2):
                            pool.wait_ge(s["rsum_ready"], count("rsum_ready", n, 2 * k + e + 1))
                            pe_ = probs[:, k % 2, e, PAD:PAD + gn * KW].rearrange("p (h k) -> p h k", k=KW)
                            nc.gpsimd.tensor_tensor(
                                pe_, pe_, rsums[:, k % 2, e, 0:gn].unsqueeze(2).to_broadcast([P, gn, KW]),
                                ALU.mult).then_inc(s["pn_ready"], 1)
            rows(pool, layer_start, iteration)

        @block.scalar
        def _(act):
            s = sems
            start_ahead(act, "act")
            act.wait_ge(setup, 7)
            act.wait_ge(consts_in, 16 * 7)
            nc.scalar.activation(gate_t[:, :], gate[:, :], ACT.Tanh).then_inc(gate_ready, 1)
            load_tables(nc, act, EXP_LN_TABLES)

            def iteration(A, B, C, D):
                def keep_transposed(u, e):
                    n, (t, _, gn) = B[0], GROUPS[u]
                    act.wait_ge(s["pt_done"], count("pt_done", n, 2 * u + e + 1))
                    act.wait_ge(s["o_done"], count("o_done", n, u))
                    w = gn * (KW if t else P)
                    nc.scalar.activation(probsT[:, e, 0:w], b_pt[:, 0:w], ACT.Copy).then_inc(s["pt_kept"], 1)

                def inverse_norms(k):
                    n = A[0]
                    act.wait_ge(s["norm_done"], count("norm_done", n, k + 1))
                    act.wait_ge(s["rnorm_ready"], count("rnorm_ready", n, k))
                    nc.scalar.activation(ln_n2[:, :], b_nv[:, :], ACT.Ln, bias=eps_c[:, 1:2],
                                         scale=LN_SCALE).then_inc(s["ln_ready"], 1)
                    act.wait_ge(s["ln_ready"], count("ln_ready", n, k + 1))
                    act.wait_ge(s["rot_ready"], count("rot_ready", n, k - 1))
                    nc.scalar.activation(rnorm[:, k % 2, :], ln_n2[:, :], ACT.Exp, bias=eps_c[:, 2:3],
                                         scale=-0.5).then_inc(s["rnorm_ready"], 1)

                for k in range(STEPS):
                    if C and k == 4:
                        n = C[0]
                        act.wait_ge(s["var_done"], count("var_done", n, 1))
                        act.wait_ge(s["rstd_ready"], count("rstd_ready", n, 1, back=1))
                        nc.scalar.activation(ln_v[:, :], b_c[:, 0:S], ACT.Ln, bias=eps_c[:, 0:1]
                                             ).then_inc(s["lnv_ready"], 1)
                        act.wait_ge(s["lnv_ready"], count("lnv_ready", n, 1))
                        act.wait_ge(s["xn_ready"], count("xn_ready", n, 1, back=1))
                        nc.scalar.activation(rstd[:, :], ln_v[:, :], ACT.Exp, scale=-0.5).then_inc(s["rstd_ready"], 1)
                    if B and 2 <= k < len(GROUPS) + 2:
                        keep_transposed(k - 2, 0)
                    if A:
                        n = A[0]
                        act.wait_ge(s["qk_done"], count("qk_done", n, k + 1))
                        act.wait_ge(s["norm_done"], count("norm_done", n, k - 1))
                        nc.scalar.activation(sq[:, k % 2, :], b_qk[k % 2][:, :], ACT.Square).then_inc(s["sq_ready"], 1)
                    if B and 2 <= k < len(GROUPS) + 2:
                        keep_transposed(k - 2, 1)
                    if A and k >= 1:
                        inverse_norms(k - 1)
                    if B and k < len(GROUPS):
                        n, gn = B[0], GROUPS[k][2]
                        for e in range(2):
                            act.wait_ge(s["max_ready"], count("max_ready", n, 2 * k + e + 1))
                            act.wait_ge(s["pt_done"], count("pt_done", n, 2 * k + e - 3))
                            for h in range(gn):
                                last = nc.scalar.activation(
                                    probs[:, k % 2, e, PAD + h * KW:PAD + (h + 1) * KW], b_sc[e][:, h * KW:(h + 1) * KW],
                                    ACT.Exp, bias=nmax[:, e, h:h + 1], accum_out=psums[:, k % 2, e, h:h + 1])
                            last.then_inc(s["exp_ready"], 1)
                    if A and k >= len(GROUPS):
                        n, _, p, loaded = A
                        act.wait_ge(s["o_done"], count("o_done", n, 6, back=2))
                        for e in range(2):
                            i = 2 * (k - len(GROUPS)) + e
                            act.wait_ge(s["v_done"], count("v_done", n, i + 1))
                            nc.scalar.activation(v[:, p, i // 2, e * 512:(e + 1) * 512], b_sc[e][:, :],
                                                 ACT.Copy).then_inc(s["v_kept"], 1)
                if A:
                    inverse_norms(STEPS - 1)
                if C:
                    n = C[0]
                    act.wait_ge(s["h_kept"], count("h_kept", n, 3))
                    act.wait_ge(s["hh_ready"], count("hh_ready", n, 1, back=1))
                    nc.scalar.activation(gg[:, :], gt[:, :], ACT.Gelu).then_inc(s["gelu_ready"], 1)
                    load_tables(nc, act, EXP_LN_TABLES)
            rows(act, lambda layer: None, iteration)

        @block.vector
        def _(dve):
            s = sems
            start_ahead(dve, "dve")
            dve.wait_ge(consts_in, 16 * 7)
            for i in range(GMAX):
                nc.vector.tensor_copy(lmask[:, :, i, :], lmask_f[:, :].rearrange("p (t k) -> p t k", t=2)
                                      ).then_inc(setup2, 1)
            dve.wait_ge(setup2, GMAX)

            def layer_start(layer):
                dve.wait_ge(tab_ready, 4 * layer + 4)

            def iteration(A, B, C, D):
                def keep_o(u):
                    n, (t, j0, gn) = B[0], GROUPS[u]
                    dve.wait_ge(s["o_done"], count("o_done", n, u + 1))
                    dve.wait_ge(s["wo_done"], count("wo_done", n, 1, back=1))
                    nc.vector.tensor_copy(oT[:, j0:j0 + gn, t * P:(t + 1) * P],
                                          b_o[:, 0:gn * P].rearrange("p (j t) -> p j t", j=gn)
                                          ).then_inc(s["o_kept"], 1)

                def rotate(k):
                    n, _, p, loaded = A
                    dve.wait_ge(s["rnorm_ready"], count("rnorm_ready", n, k + 1))
                    dve.wait_ge(s["sum_ready"], count("sum_ready", n, k + 1))
                    dve.wait_ge(s["scores_done"], count("scores_done", n, 12, back=2))
                    j = 2 * (k % 4)
                    if k < 4:
                        parts = [(slice(0, P), qT[:, p, j:j + 2, :])]
                    else:
                        parts = [(slice(e * DH, (e + 1) * DH),
                                  kT[e * DH:(e + 1) * DH, p, e, j:j + 2, WIN:WIN + S]) for e in range(2)]
                    for r, dst in parts:
                        last = nc.vector.scalar_tensor_tensor(
                            out=dst, in0=rnorm[r, k % 2, :].rearrange("p (j t) -> p j t", j=2), scalar=1e12,
                            in1=rot_c[r, k % 2, :].rearrange("p (j t) -> p j t", j=2), op0=ALU.min, op1=ALU.mult)
                    last.then_inc(s["rot_ready"], 1)

                for k in range(STEPS):
                    if B and 3 <= k < len(GROUPS) + 3:
                        keep_o(k - 3)
                    if D and k == 0:
                        n = D[0]
                        dve.wait_ge(s["gelu_ready"], count("gelu_ready", n, 1))
                        dve.wait_ge(s["h_kept"], count("h_kept", n, 6))
                        dve.wait_ge(s["w2_done"], count("w2_done", n, 1, back=1))
                        nc.vector.tensor_tensor(hT[:, :], at[:, :], gg[:, :], ALU.mult).then_inc(s["hh_ready"], 1)
                    if D and k == 1:
                        n, b, _, _ = D
                        dve.wait_ge(s["w2_done"], count("w2_done", n, 1))
                        nc.vector.scalar_tensor_tensor(out=xT[:, b, :], in0=b_c[:, 0:S], scalar=par[:, P_B2:P_B2 + 1],
                                                       in1=x1[:, :], op0=ALU.add, op1=ALU.add
                                                       ).then_inc(s["x_ready"], 1)
                    if C:
                        n, b, _, loaded = C
                        if k == 2:
                            dve.wait_ge(s["wo_done"], count("wo_done", n, 1))
                            dve.wait_ge(s["x_ready"], count("x_ready", n, 1, back=1))
                            nc.vector.tensor_tensor(x1[:, :], b_c[:, 0:S], xT[:, b, :], ALU.add
                                                    ).then_inc(s["x1_ready"], 1)
                        if k == 3:
                            dve.wait_ge(s["mu_done"], count("mu_done", n, 1))
                            dve.wait_ge(s["xs1_ready"], count("xs1_ready", n, 2))
                            nc.vector.tensor_tensor(xc[:, :], xs1[:, :], b_c[:, S:2 * S], ALU.subtract
                                                    ).then_inc(s["xc_ready"], 1)
                            dve.wait_ge(s["xc_ready"], count("xc_ready", n, 1))
                            nc.vector.tensor_tensor(xsq[:, :], xc[:, :], xc[:, :], ALU.mult
                                                    ).then_inc(s["xsq_ready"], 1)
                        if k == 4:
                            dve.wait_ge(vectors_in, loaded)
                            dve.wait_ge(s["rstd_ready"], count("rstd_ready", n, 1))
                            nc.vector.tensor_tensor(xn[:, :], xc[:, :], rstd[:, :], ALU.mult
                                                    ).then_inc(s["xn_ready"], 1)
                            dve.wait_ge(s["xn_ready"], count("xn_ready", n, 1))
                            nc.vector.tensor_scalar(xg[:, :], xn[:, :], par[:, P_G:P_G + 1], par[:, P_B:P_B + 1],
                                                    ALU.mult, ALU.add).then_inc(s["xg_ready"], 1)
                        if 5 <= k <= 7:
                            dve.wait_ge(s["h_done"], count("h_done", n, k - 4))
                            for i in (2 * k - 10, 2 * k - 9):
                                dst = gt if i < FB else at
                                nc.vector.tensor_scalar(dst[:, (i % FB) * S:(i % FB + 1) * S],
                                                        b_c[:, (i % 2) * S:(i % 2 + 1) * S],
                                                        par[:, P_B1 + i:P_B1 + i + 1], None, ALU.add
                                                        ).then_inc(s["h_kept"], 1)
                    if B and 1 <= k <= len(GROUPS):
                        u = k - 1
                        n, gn = B[0], GROUPS[u][2]
                        for e in range(2):
                            dve.wait_ge(s["exp_ready"], count("exp_ready", n, 2 * u + e + 1))
                            dve.wait_ge(s["pn_ready"], count("pn_ready", n, 2 * u + e - 3))
                            nc.vector.reciprocal(rsums[:, u % 2, e, 0:gn], psums[:, u % 2, e, 0:gn]).then_inc(s["rsum_ready"], 1)
                    if A:
                        n = A[0]
                        tab = 0 if k < 4 else 2
                        def per_block(x):
                            return x.rearrange("p (j t) -> p j t", j=2)
                        dve.wait_ge(s["sq_ready"], count("sq_ready", n, k + 1))
                        wait_apart(dve, dve_passed, s["sum_ready"], count("sum_ready", n, k - 1))
                        nc.vector.stream_shuffle(rot_s[:, k % 2, :], b_qk[k % 2][:, :], [i ^ 1 for i in range(32)]
                                                 ).then_inc(s["shuf_ready"], 1)
                        dve.wait_ge(s["rot_ready"], count("rot_ready", n, k - 1))
                        nc.vector.tensor_tensor(
                            per_block(rot_c[:, k % 2, :]), per_block(b_qk[k % 2][:, :]),
                            rot_tab[:, tab, :].unsqueeze(1).to_broadcast([P, 2, S]), ALU.mult
                        ).then_inc(s["rotc_ready"], 1)
                        dve.wait_ge(s["shuf_ready"], count("shuf_ready", n, k + 1))
                        nc.vector.tensor_tensor(
                            per_block(rot_s[:, k % 2, :]), per_block(rot_s[:, k % 2, :]),
                            rot_tab[:, tab + 1, :].unsqueeze(1).to_broadcast([P, 2, S]), ALU.mult
                        ).then_inc(s["rots_ready"], 1)
                    if B and k < len(GROUPS):
                        n, gn = B[0], GROUPS[k][2]
                        for e in range(2):
                            dve.wait_ge(s["scores_done"], count("scores_done", n, 2 * k + e + 1))
                            dve.wait_ge(s["exp_ready"], count("exp_ready", n, 2 * k + e - 1))
                            nc.vector.tensor_reduce(
                                nmax[:, e, 0:gn], b_sc[e][:, 0:gn * KW].rearrange("p (h k) -> p h k", k=KW),
                                AX_X, ALU.max, negate=True).then_inc(s["max_ready"], 1)
                    if A:
                        dve.wait_ge(s["rotc_ready"], count("rotc_ready", A[0], k + 1))
                        dve.wait_ge(s["rots_ready"], count("rots_ready", A[0], k + 1))
                        nc.vector.tensor_tensor(rot_c[:, k % 2, :], rot_c[:, k % 2, :], rot_s[:, k % 2, :], ALU.add
                                                ).then_inc(s["sum_ready"], 1)
                        if k >= 1:
                            rotate(k - 1)
                if B:
                    keep_o(len(GROUPS) - 1)
                if A:
                    rotate(STEPS - 1)
            rows(dve, layer_start, iteration)
            dve.wait_ge(gate_ready, 1)
            dve.wait_ge(s["x_ready"], count("x_ready", DEPTH * NB, 0))
            with dve.Fori(0, NB) as b:
                nc.vector.scalar_tensor_tensor(out=xT[:, b, :], in0=xT[:, b, :], scalar=gate_t[:, 0:1],
                                               in1=xres[:, b, :], op0=ALU.mult, op1=ALU.add).then_inc(fin_ready, 1)

        @block.tensor
        def _(pe):
            s = sems
            start_ahead(pe, "pe")
            pe.wait_ge(setup2, GMAX)
            pe.wait_ge(setup, 7)

            def iteration(A, B, C, D):
                def norms(k):
                    n = A[0]
                    pe.wait_ge(s["sq_ready"], count("sq_ready", n, k + 1))
                    pe.wait_ge(s["ln_ready"], count("ln_ready", n, k))
                    nc.tensor.matmul(b_nv[:, :], pair_ones[:, :], sq[:, k % 2, :], start=True, stop=True
                                     ).then_inc(s["norm_done"], 1)

                for k in range(STEPS):
                    def transposes(e):
                        u = k - 2
                        n, (t, _, gn) = B[0], GROUPS[u]
                        pe.wait_ge(s["pn_ready"], count("pn_ready", n, 2 * u + e + 1))
                        pe.wait_ge(s["pt_kept"], count("pt_kept", n, 2 * u + e))
                        for h in range(gn):
                            c0 = PAD + h * KW
                            last = nc.tensor.transpose(b_pt[:, h * P:(h + 1) * P], probs[:, u % 2, e, c0 + WIN:c0 + KW],
                                                       ident[:, :])
                        if t:
                            for h in range(gn):
                                c0 = PAD + h * KW
                                o0 = gn * P + h * WIN
                                last = nc.tensor.transpose(b_pt[:, o0:o0 + WIN], probs[0:WIN, u % 2, e, c0 + WIN - P:c0 + WIN],
                                                           ident[0:WIN, 0:WIN])
                        last.then_inc(s["pt_done"], 1)

                    if B and 2 <= k < len(GROUPS) + 2:
                        transposes(0)
                    if A and k >= 1:
                        norms(k - 1)
                    if A:
                        n, _, p, loaded = A
                        pe.wait_ge(s["xs_ready"], count("xs_ready", n, 2))
                        pe.wait_ge(part_in[PART_Q if k < 4 else PART_K], loaded)
                        pe.wait_ge(s["rotc_ready"], count("rotc_ready", n, k - 1))
                        for i in range(2):
                            c0 = W_QK + (2 * k + i) * P
                            last = nc.tensor.matmul(b_qk[k % 2][:, i * S:(i + 1) * S], weights[:, c0:c0 + P],
                                                    xs[:, p, :], start=True, stop=True)
                        last.then_inc(s["qk_done"], 1)
                    if B and 2 <= k < len(GROUPS) + 2:
                        transposes(1)
                    if B and k < len(GROUPS):
                        n, _, p, loaded = B
                        t, j0, gn = GROUPS[k]
                        pe.wait_ge(s["v_kept"], count("v_kept", n, 4))
                        pe.wait_ge(s["rot_ready"], count("rot_ready", n, STEPS // 2 + (j0 + gn + 1) // 2))
                        for e in range(2):
                            pe.wait_ge(s["exp_ready"], count("exp_ready", n, 2 * k + e - 1))
                            nc.tensor.matmul(b_sc[e][:, 0:gn * KW], identb[:, :],
                                             lmask[:, t, 0:gn, :], start=True, stop=False,
                                             skip_group_check=True)
                        for h in range(gn):
                            for e in range(2):
                                last = nc.tensor.matmul(
                                    b_sc[e][:, h * KW:(h + 1) * KW], qT[:, p, j0 + h, t * P:(t + 1) * P],
                                    kT[:, p, e, j0 + h, t * P:t * P + KW], start=False, stop=(h == gn - 1),
                                    skip_group_check=True)
                                if h == gn - 1:
                                    last.then_inc(s["scores_done"], 1)
                    if A and k >= len(GROUPS):
                        n, _, p, loaded = A
                        pe.wait_ge(part_in[PART_V], loaded)
                        pe.wait_ge(s["exp_ready"], count("exp_ready", n, 12, back=1))
                        for e in range(2):
                            i = 2 * (k - len(GROUPS)) + e
                            pe.wait_ge(s["v_kept"], count("v_kept", n, i - 1))
                            nc.tensor.matmul(b_sc[e][:, :], xs[:, p, (i // 2) * P:(i // 2 + 1) * P],
                                             weights[:, W_V + e * 512:W_V + (e + 1) * 512],
                                             start=True, stop=True).then_inc(s["v_done"], 1)
                    if D and k == 0:
                        n, loaded = D[0], D[3]
                        pe.wait_ge(part_in[PART_2], loaded)
                        pe.wait_ge(s["hh_ready"], count("hh_ready", n, 1))
                        for i in range(FB):
                            last = nc.tensor.matmul(b_c[:, 0:S], weights[:, W_2 + i * P:W_2 + (i + 1) * P],
                                                    hT[:, i * S:(i + 1) * S], start=(i == 0), stop=(i == FB - 1))
                        last.then_inc(s["w2_done"], 1)
                    if B and 2 <= k < len(GROUPS) + 2:
                        u = k - 2
                        n, _, p, loaded = B
                        t, j0, gn = GROUPS[u]
                        pe.wait_ge(s["v_kept"], count("v_kept", n, 4))
                        pe.wait_ge(s["o_kept"], count("o_kept", n, u))
                        pe.wait_ge(s["pt_kept"], count("pt_kept", n, 2 * u + 2))
                        for h in range(gn):
                            for e in range(2):
                                r = slice(e * DH, (e + 1) * DH)
                                vc = slice((2 * (j0 + h) + e) * DH, (2 * (j0 + h) + e + 1) * DH)
                                last = nc.tensor.matmul(b_o[r, h * P:(h + 1) * P], v[:, p, t, vc],
                                                        probsT[:, e, h * P:(h + 1) * P], start=True, stop=(t == 0),
                                                        skip_group_check=True)
                            if t:
                                for e in range(2):
                                    r = slice(e * DH, (e + 1) * DH)
                                    vc = slice((2 * (j0 + h) + e) * DH, (2 * (j0 + h) + e + 1) * DH)
                                    c0 = gn * P + h * WIN
                                    last = nc.tensor.matmul(
                                        b_o[r, h * P:h * P + WIN], v[P - WIN:P, p, 0, vc],
                                        probsT[P - WIN:P, e, c0:c0 + WIN], start=False, stop=True,
                                        skip_group_check=True)
                        last.then_inc(s["o_done"], 1)

                    if C:
                        n, loaded = C[0], C[3]
                        if k == 1:
                            pe.wait_ge(part_in[PART_O], loaded)
                            pe.wait_ge(s["o_kept"], count("o_kept", n, 6))
                            pe.wait_ge(s["x_ready"], count("x_ready", n, 1, back=1))
                            for j in range(NJ):
                                last = nc.tensor.matmul(b_c[:, 0:S], weights[:, W_O + j * P:W_O + (j + 1) * P],
                                                        oT[:, j, :], start=(j == 0), stop=(j == NJ - 1))
                            last.then_inc(s["wo_done"], 1)
                        if k == 2:
                            pe.wait_ge(s["xs1_ready"], count("xs1_ready", n, 2))
                            nc.tensor.matmul(b_c[:, S:2 * S], mean_mat[:, :], xs1[:, :], start=True, stop=True
                                             ).then_inc(s["mu_done"], 1)
                        if k == 3:
                            pe.wait_ge(s["xsq_ready"], count("xsq_ready", n, 1))
                            nc.tensor.matmul(b_c[:, 0:S], mean_mat[:, :], xsq[:, :], start=True, stop=True
                                             ).then_inc(s["var_done"], 1)
                        if 4 <= k <= 6:
                            pe.wait_ge(part_in[PART_1], loaded)
                            pe.wait_ge(s["xg_ready"], count("xg_ready", n, 1))
                            pe.wait_ge(s["h_kept"], count("h_kept", n, 2 * k - 8))
                            for i in (2 * k - 8, 2 * k - 7):
                                last = nc.tensor.matmul(b_c[:, (i % 2) * S:(i % 2 + 1) * S],
                                                        weights[:, W_1 + i * P:W_1 + (i + 1) * P], xg[:, :],
                                                        start=True, stop=True)
                            last.then_inc(s["h_done"], 1)
                if A:
                    norms(STEPS - 1)
            rows(pe, lambda layer: None, iteration)


def build(nc, ins, out, NB, DEPTH):
    with ExitStack() as ctx:
        ident = ctx.enter_context(nc.sbuf_tensor("ident", [P, P], F32))
        identb = ctx.enter_context(nc.sbuf_tensor("identb", [P, P], BF16))
        x1_scr = nc.dram_tensor("x1_scr", [P, NB, S], F32, kind="Internal").ap()
        xn_scr = nc.dram_tensor("xn_scr", [P, NB, S], F32, kind="Internal").ap()
        ident_ready = ctx.enter_context(nc.semaphore("ident_ready"))
        with nc.Block() as block:
            @block.gpsimd
            def _(pool):
                for m in (ident, identb):
                    nc.gpsimd.memset(m[:, :], 0.0).then_inc(ident_ready, 1)
                pool.wait_ge(ident_ready, 2)
                for m in (ident, identb):
                    nc.gpsimd.affine_select(out=m[:, :], in_=m[:, :], compare_op=ALU.not_equal, fill=1.0, base=0,
                                            pattern=[[-1, P]], channel_multiplier=1).then_inc(ident_ready, 1)
                pool.wait_ge(ident_ready, 4)
        cross_phase(nc, x1_scr, xn_scr, ident, identb, ins, NB)
        ffn_phase(nc, xn_scr, x1_scr, ident, identb, ins, out, NB, DEPTH)




def rotary_tables():
    f = np.float32
    half = np.arange(0, DH, 2, dtype=f)
    inv_freq = (f(1.0) / f(10000.0) ** (half / f(DH))).astype(f)
    t = np.arange(S, dtype=f)
    freqs = (t[:, None] * inv_freq[None, :]).astype(f)
    base = ((half + f(0.4 * DH)) / f(1.4 * DH)).astype(f)
    power = (t - f(S // 2)) / f(WIN // 2)
    scale = (base[None, :] ** power[:, None]).astype(f)
    cos, sin = np.cos(freqs.astype(np.float64)), np.sin(freqs.astype(np.float64))
    out = np.zeros((4, 2, DH // 2, 2, S), f)
    for i, sc in ((0, f(QK_SCALE) * scale), (2, f(1.0) / scale)):
        for hf, sign in ((0, -1.0), (1, 1.0)):
            out[i, :, :, hf] = (cos * sc).T
            out[i + 1, :, :, hf] = (sign * sin * sc).T
    return np.ascontiguousarray(out.reshape(4, P, S).transpose(1, 0, 2))


def local_constants():
    q = np.arange(P)[:, None]
    c = np.arange(KW)[None, :]
    mask = np.zeros((P, 2, KW), np.float32)
    for t in range(2):
        i, j = t * P + q, t * P - WIN + c
        window = (j // WIN == i // WIN) | (j // WIN == i // WIN - 1)
        seen = window & (j >= 0) & (i >= j) & (i <= j + WIN)
        mask[:, t, :] = np.where(seen, 0.0, -BIG)
    ones = np.kron(np.eye(2), np.ones((DH, DH))).astype(np.float32)
    return np.concatenate([mask.reshape(P, 2 * KW), ones, np.full((P, P), 1.0 / P, np.float32)], 1)


def interleave(w):
    return np.swapaxes(w.reshape(*w.shape[:-1], -1, 2, DH // 2), -1, -2).reshape(w.shape)


def swap_pairs(w):
    return w.reshape(*w.shape[:-1], -1, 2)[..., ::-1].reshape(w.shape)


def layer_weights(Wqkv, Wo, W1, W2):
    L = Wqkv.shape[0]
    out = np.zeros((L, P, W_END), np.float32)
    out[:, :, W_QK:W_V] = interleave(Wqkv[:, :, :2 * INNER])
    out[:, :, W_V:W_O] = Wqkv[:, :, 2 * INNER:]
    out[:, :, W_O:W_1] = Wo.reshape(L, NJ, P, P).transpose(0, 2, 1, 3).reshape(L, P, INNER)
    out[:, :, W_1:W_1 + FFN] = W1[:, :, FFN:]
    out[:, :, W_1 + FB * P:W_1 + FB * P + FFN] = W1[:, :, :FFN]
    w2 = np.zeros((L, FB * P, P), np.float32)
    w2[:, :FFN] = W2
    out[:, :, W_2:W_END] = w2.reshape(L, FB, P, P).transpose(0, 2, 1, 3).reshape(L, P, FB * P)
    return out


def layer_vectors(q_scale, k_scale, ln_g, ln_b, b1, b2):
    L = q_scale.shape[0]
    out = np.zeros((L, P, N_PAR), np.float32)
    q_scale, k_scale = interleave(q_scale), interleave(k_scale)
    for col, vec in ((P_Q, q_scale), (P_QR, swap_pairs(q_scale)), (P_K, k_scale), (P_KR, swap_pairs(k_scale))):
        out[:, :, col] = np.concatenate([vec, vec], 1)
    out[:, :, P_G], out[:, :, P_B], out[:, :, P_B2] = ln_g, ln_b, b2
    b = np.zeros((L, 2, FB * P), np.float32)
    b[:, 0, :FFN], b[:, 1, :FFN] = b1[:, FFN:], b1[:, :FFN]
    out[:, :, P_B1:] = b.reshape(L, 2 * FB, P).transpose(0, 2, 1)
    return out


def cross_weights(w_q, w_k, w_v, w_o):
    out = np.zeros((P, X_END), np.float32)
    out[:, XW_Q:XW_K], out[:, XW_K:XW_V], out[:, XW_V:XW_O] = w_q, w_k, w_v
    wo = np.zeros((4, 4, 32, P), np.float32)
    wo[:, :, :DK] = w_o.reshape(4, 4, DK, P)
    out[:, XW_O:XW_M] = wo.reshape(4, P, P).transpose(1, 0, 2).reshape(P, 4 * P)
    out[:, XW_M:XW_S] = 1.0 / P
    for h in range(4):
        out[32 * h + DK, XW_S + 32 * h:XW_S + 32 * h + 32] = 1.0
    return out


def one_more(a):
    return np.concatenate([a, np.zeros_like(a[:1])])


def cross_inputs(x, ctx, mask, g, w_q, b_q, w_k, b_k, w_v, b_v, w_o, b_o):
    m = one_more(mask[:, 0])
    return dict(
        xin=np.ascontiguousarray(x.transpose(2, 0, 1)), ctx=np.ascontiguousarray(one_more(ctx).transpose(2, 0, 1)),
        mask_q=m, mask_k=np.ascontiguousarray(m.transpose(0, 2, 1)), x_w=cross_weights(w_q, w_k, w_v, w_o),
        x_vec=np.stack([b_q, b_k, b_o, np.broadcast_to(g, (P,))], 1).astype(np.float32),
        bv=np.ascontiguousarray(np.broadcast_to(b_v, (P, P))))

def kernel(x, ctx_1024, mask_Bx1xSxS2_bk1, g_xattn, g_ffn, L0_xattn_w_q, L0_xattn_b_q, L0_xattn_w_k, L0_xattn_b_k,
           L0_xattn_w_v, L0_xattn_b_v, L0_xattn_w_o, L0_xattn_b_o, L0_ffn_Wqkv, L0_ffn_q_scale, L0_ffn_k_scale,
           L0_ffn_Wo, L0_ffn_ln_g, L0_ffn_ln_b, L0_ffn_W1, L0_ffn_b1, L0_ffn_W2, L0_ffn_b2):
    import concourse.bacc as bacc
    from concourse.bass_utils import run_bass_kernel_spmd

    NB, DEPTH = x.shape[0], L0_ffn_Wqkv.shape[0]
    arrays = cross_inputs(x, ctx_1024, mask_Bx1xSxS2_bk1, g_xattn, L0_xattn_w_q, L0_xattn_b_q, L0_xattn_w_k,
                          L0_xattn_b_k, L0_xattn_w_v, L0_xattn_b_v, L0_xattn_w_o, L0_xattn_b_o)
    arrays.update(ffn_w=layer_weights(L0_ffn_Wqkv, L0_ffn_Wo, L0_ffn_W1, L0_ffn_W2),
                  ffn_vec=layer_vectors(L0_ffn_q_scale, L0_ffn_k_scale, L0_ffn_ln_g, L0_ffn_ln_b, L0_ffn_b1, L0_ffn_b2),
                  rot=rotary_tables(), lmask=local_constants(),
                  gate_f=np.ascontiguousarray(np.broadcast_to(g_ffn, (P, 1))))
    arrays = {f"in_{name}": a for name, a in arrays.items()}
    nc = bacc.Bacc("TRN2", target_bir_lowering=False, num_devices=1)
    ins = {name[3:]: nc.dram_tensor(name, a.shape, mybir.dt.from_np(a.dtype), kind="ExternalInput").ap()
           for name, a in arrays.items()}
    out = nc.dram_tensor("out", (P, NB, S), F32, kind="ExternalOutput").ap()
    build(nc, ins, out, NB, DEPTH)
    r = run_bass_kernel_spmd(nc, [arrays], core_ids=[0])
    return np.ascontiguousarray(r.results[0]["out"].transpose(1, 2, 0))
```
